# Optimizing a Trainium2 kernel written in Bass

```python
import numpy as np
import jax
import jax.numpy as jnp

def _softmax(x, axis=-1):
    return jax.nn.softmax(x, axis=axis)

def _gelu(x):
    return jax.nn.gelu(x, approximate=True)

def _silu(x):
    return jax.nn.silu(x)

def _sigmoid(x):
    return jax.nn.sigmoid(x)

def _layernorm(x, axis=-1, eps=1e-05):
    m = jnp.mean(x, axis=axis, keepdims=True)
    v = jnp.var(x, axis=axis, keepdims=True)
    return (x - m) / jnp.sqrt(v + eps)

def _scatter_add(tgt, idx, src, axis=0):
    return tgt.at[idx].add(src)

def _segment_sum(src, seg, n):
    return jax.ops.segment_sum(src, seg, n)
kernel_name = 'mk_prb_d1_jaxref_r8_49486a'

def setup_inputs(seed: int=0):
    np.random.seed(seed)
    _w = jnp.asarray

    def _L0_attn_setup():
        import jax, jax.numpy as jnp
        import numpy as np
        B, T, H, S, F, G = (2, 256, 512, 128, 1248, 6)
        GRAD_ORDER_MIN = 4
        THD = 2.5
        key = jax.random.key(seed)
        ks = jax.random.split(key, 9)
        sc = 0.02
        hidden_states = jax.random.normal(ks[0], (B, T, H), jnp.float32)
        up_w = jax.random.normal(ks[1], (S, H), jnp.float32) * sc
        gate_w = jax.random.normal(ks[2], (S, H), jnp.float32) / np.sqrt(H)
        local_point = jax.random.normal(ks[3], (S,), jnp.float32)
        local_approx_output = jax.random.normal(ks[4], (H, S), jnp.float32) * sc
        fuse_weight = jax.random.normal(ks[5], (H, S, G), jnp.float32) * sc
        discount_factor = jnp.asarray(np.cumsum(np.log(np.arange(1, G + 1, dtype=np.float64))), jnp.float32)
        ffn_gate_w = jax.random.normal(ks[6], (F, H), jnp.float32) * sc
        ffn_up_w = jax.random.normal(ks[7], (F, H), jnp.float32) * sc
        ffn_down_w = jax.random.normal(ks[8], (H, F), jnp.float32) * sc
        return {'hidden_states': hidden_states, 'up_w': up_w, 'gate_w': gate_w, 'local_point': local_point, 'local_approx_output': local_approx_output, 'fuse_weight': fuse_weight, 'discount_factor': discount_factor, 'ffn_gate_w': ffn_gate_w, 'ffn_up_w': ffn_up_w, 'ffn_down_w': ffn_down_w}
    _L0_attn_in = _L0_attn_setup()

    def _L0_ffn_setup():
        import jax, jax.numpy as jnp
        import numpy as np
        import math
        SQRT7 = math.sqrt(7.0)
        EPS = 1e-05

        def int4_quant(x):
            beta = jnp.mean(jnp.abs(x), axis=-1, keepdims=True)
            x_q = jnp.clip(jnp.round(x * SQRT7 / (beta + EPS)), -8, 7)
            return x_q * (beta * SQRT7) / SQRT7

        def int8_quant(x):
            gamma = jnp.max(jnp.abs(x), axis=-1, keepdims=True)
            x_q = jnp.clip(jnp.round(x * 127.0 / (gamma + EPS)), -128, 127)
            return x_q * gamma / 127.0

        def bitlinear(x, w, scale):
            w_mean = jnp.mean(jnp.abs(w))
            w_q = jnp.clip(jnp.round(w / (w_mean + EPS)), -1.0, 1.0)
            w_eff = w_q * w_mean * scale
            return jnp.einsum('...i,oi->...o', x, w_eff)
        key = jax.random.key(seed)
        ks = jax.random.split(key, 4)
        H, I = (512, 1376)
        B, S = (2, 256)
        x = jax.random.normal(ks[0], (B, S, H), dtype=jnp.float32)
        w_gate = jax.random.uniform(ks[1], (I, H), jnp.float32, -1.0, 1.0) / np.sqrt(H)
        w_up = jax.random.uniform(ks[2], (I, H), jnp.float32, -1.0, 1.0) / np.sqrt(H)
        w_down = jax.random.uniform(ks[3], (H, I), jnp.float32, -1.0, 1.0) / np.sqrt(I)
        ones = jnp.ones((1,), jnp.float32)
        return {'x': x, 'w_gate': w_gate, 'w_up': w_up, 'w_down': w_down, 's_gate': ones, 's_up': ones, 's_down': ones}
    _L0_ffn_in = _L0_ffn_setup()
    _d = {'L0_attn_hidden_states': _L0_attn_in['hidden_states'], 'L0_attn_up_w': _L0_attn_in['up_w'], 'L0_attn_gate_w': _L0_attn_in['gate_w'], 'L0_attn_local_point': _L0_attn_in['local_point'], 'L0_attn_local_approx_output': _L0_attn_in['local_approx_output'], 'L0_attn_fuse_weight': _L0_attn_in['fuse_weight'], 'L0_attn_discount_factor': _L0_attn_in['discount_factor'], 'L0_attn_ffn_gate_w': _L0_attn_in['ffn_gate_w'], 'L0_attn_ffn_up_w': _L0_attn_in['ffn_up_w'], 'L0_attn_ffn_down_w': _L0_attn_in['ffn_down_w'], 'L0_ffn_w_gate': _L0_ffn_in['w_gate'], 'L0_ffn_w_up': _L0_ffn_in['w_up'], 'L0_ffn_w_down': _L0_ffn_in['w_down'], 'L0_ffn_s_gate': _L0_ffn_in['s_gate'], 'L0_ffn_s_up': _L0_ffn_in['s_up'], 'L0_ffn_s_down': _L0_ffn_in['s_down']}
    _x0 = _d['L0_attn_hidden_states']
    _d['L0_attn_hidden_states'] = jax.random.normal(jax.random.fold_in(jax.random.key(seed), 1), (2, 1024, 512), dtype=_x0.dtype)
    del _x0
    return _d

def reference(L0_attn_hidden_states, L0_attn_up_w, L0_attn_gate_w, L0_attn_local_point, L0_attn_local_approx_output, L0_attn_fuse_weight, L0_attn_discount_factor, L0_attn_ffn_gate_w, L0_attn_ffn_up_w, L0_attn_ffn_down_w, L0_ffn_w_gate, L0_ffn_w_up, L0_ffn_w_down, L0_ffn_s_gate, L0_ffn_s_up, L0_ffn_s_down):

    def _L0_attn_ref(hidden_states, up_w, gate_w, local_point, local_approx_output, fuse_weight, discount_factor, ffn_gate_w, ffn_up_w, ffn_down_w):
        import jax, jax.numpy as jnp
        import numpy as np
        B, T, H, S, F, G = (2, 256, 512, 128, 1248, 6)
        GRAD_ORDER_MIN = 4
        THD = 2.5
        approx_up = hidden_states @ up_w.T
        gate_pre = hidden_states @ gate_w.T
        delta = gate_pre - local_point
        neg_factor = jnp.where(delta > 0, 1.0, -1.0).astype(hidden_states.dtype)
        delta_abs = jnp.abs(delta)
        log_delta = jnp.log(delta_abs)
        keep = (delta_abs <= THD).astype(hidden_states.dtype)
        approx_out = approx_up @ local_approx_output.T
        for idx in range(G):
            m = idx + 1
            dterm = jnp.exp(log_delta * m - discount_factor[idx])
            if m % 2 == 1:
                dterm = dterm * neg_factor
            tmp = dterm * approx_up
            if m > GRAD_ORDER_MIN:
                tmp = tmp * keep
            approx_out = approx_out + tmp @ fuse_weight[:, :, idx].T
        ffn_out = jax.nn.silu(hidden_states @ ffn_gate_w.T) * (hidden_states @ ffn_up_w.T) @ ffn_down_w.T
        return approx_out + ffn_out

    def _L0_ffn_ref(x, w_gate, w_up, w_down, s_gate, s_up, s_down):
        import jax, jax.numpy as jnp
        import numpy as np
        import math
        SQRT7 = math.sqrt(7.0)
        EPS = 1e-05

        def int4_quant(x):
            beta = jnp.mean(jnp.abs(x), axis=-1, keepdims=True)
            x_q = jnp.clip(jnp.round(x * SQRT7 / (beta + EPS)), -8, 7)
            return x_q * (beta * SQRT7) / SQRT7

        def int8_quant(x):
            gamma = jnp.max(jnp.abs(x), axis=-1, keepdims=True)
            x_q = jnp.clip(jnp.round(x * 127.0 / (gamma + EPS)), -128, 127)
            return x_q * gamma / 127.0

        def bitlinear(x, w, scale):
            w_mean = jnp.mean(jnp.abs(w))
            w_q = jnp.clip(jnp.round(w / (w_mean + EPS)), -1.0, 1.0)
            w_eff = w_q * w_mean * scale
            return jnp.einsum('...i,oi->...o', x, w_eff)
        xq = int4_quant(x)
        gate = bitlinear(xq, w_gate, s_gate)
        up = bitlinear(xq, w_up, s_up)
        gate = jnp.square(jax.nn.relu(gate))
        inter = int8_quant(up * gate)
        return bitlinear(inter, w_down, s_down)
    x = L0_attn_hidden_states
    xn = _layernorm(x, axis=-1)
    x = x + _L0_attn_ref(xn, L0_attn_up_w, L0_attn_gate_w, L0_attn_local_point, L0_attn_local_approx_output, L0_attn_fuse_weight, L0_attn_discount_factor, L0_attn_ffn_gate_w, L0_attn_ffn_up_w, L0_attn_ffn_down_w) + _L0_ffn_ref(xn, L0_ffn_w_gate, L0_ffn_w_up, L0_ffn_w_down, L0_ffn_s_gate, L0_ffn_s_up, L0_ffn_s_down)
    return x

_drawn_inputs = setup_inputs


def setup_inputs(seed=0):
    import zlib

    import numpy as np

    out = dict(_drawn_inputs(seed))
    spreads = {}
    factors = {'L0_attn_local_approx_output': 2.74,
     'L0_attn_ffn_gate_w': 4.188,
     'L0_attn_ffn_up_w': 4.097,
     'L0_attn_ffn_down_w': 4.097}
    for name, (base, spread) in spreads.items():
        noise = np.random.default_rng([zlib.crc32(name.encode()), seed]).standard_normal(out[name].shape)
        drawn = base * np.exp(spread * noise) if base else spread * noise
        out[name] = jnp.asarray(drawn.astype(out[name].dtype))
    for name, factor in factors.items():
        out[name] = (out[name] * factor).astype(out[name].dtype)
    return out
```

```python
import concourse.bass as bass
from concourse import mybir
from concourse.alu_op_type import AluOpType as ALU
from contextlib import ExitStack

ACT = mybir.ActivationFunctionType
F32 = mybir.dt.float32
F16 = mybir.dt.float16
BF16 = mybir.dt.bfloat16
AX_X = mybir.AxisListType.X
RADD = bass.bass_isa.ReduceOp.add

P = 128
MAGIC = 12582912.0
LN_EPS = 1e-5
Q_EPS = 1e-5
SQRT7 = 7.0 ** 0.5
THD = 2.5
WS = 64.0
RING = 3


def spans(n, step):
    return [(o, min(step, n - o)) for o in range(0, n, step)]


def bass_kernel(nc, x, w_s, w_f, w_f_tail, w_poly, w_down, w_bg, w_bu, w_bd, local_point, scal, ident, out):
    TOK, H = x.shape
    S = local_point.shape[0]
    G = w_poly.shape[1] // H - 1
    F = w_down.shape[0]
    I = w_bg.shape[1]
    BLK = 512
    NB = TOK // BLK
    TT = BLK // P
    KC = H // P
    F_TILES = spans(F, P)
    NF = len(F_TILES)
    I_CHUNKS = spans(I, P)
    NI = len(I_CHUNKS)
    B_COLS = spans(I, 512)
    NC = len(B_COLS)
    NM = G + 1
    D_UNITS = NM + NF
    assert S == P and BLK <= 512 and H == 512 and G == 6

    PER_BLOCK = 1 + NF + TT * NC + TT
    assert PER_BLOCK % RING == 0
    FIRST_D = PER_BLOCK - TT
    STEADY = [("S", 0)]
    for n in range(max(NF, TT * NC)):
        STEADY += [("F", n)] * (n < NF) + [("B", n)] * (n < TT * NC)
    FIRST = [("S", 0)] + [("F", n) for n in range(NF)] + [("B", n) for n in range(TT * NC)]

    FRONT = 9
    XN, XQ = 4, 9
    BIT = 9
    BIT_SCALE = 7

    ctx = ExitStack()
    with ctx:
        def sb(name, shape, dt):
            return ctx.enter_context(nc.sbuf_tensor(name, shape, dt))

        def sem(name):
            return ctx.enter_context(nc.semaphore(name))

        NS = 2
        WF = sb("w_sf_split", [P, NS + 2 * NF + 1, 1024], F16)
        WD = sb("w_d_split", [P, D_UNITS + 1, 1024], F16)
        WB = sb("w_bit", [P, 2, KC * I], BF16)
        WBD = sb("w_bit_down", [P, NI, H], BF16)
        REGION = sb("region", [P, I + TT * I // 2 + NI * P // 2 + 2 * H], F32)
        o = 0
        prod = REGION[:, o:o + I]
        o += I
        q8 = REGION[:, o:o + TT * I // 2].bitcast(BF16).rearrange("p (t i) -> p t i", t=TT)
        o += TT * I // 2
        q8T = REGION[:, o:o + NI * P // 2].bitcast(BF16).rearrange("p (c t) -> p c t", c=NI)
        o += NI * P // 2
        res = REGION[:, o:o + 2 * H].rearrange("p (s h) -> p s h", s=2)
        assert max(NI * H, KC * I) <= o + 2 * H
        raw_bd = REGION[:, 0:NI * H]
        raw_bu = REGION[:, 0:KC * I]
        raw_bg = WD[:, :, :].rearrange("p u c -> p (u c)")[:, 0:2 * KC * I].bitcast(F32)

        xT_hi = sb("xT_hi", [P, KC, BLK], F16)
        xT_lo = sb("xT_lo", [P, KC, BLK], F16)
        xqT = sb("xqT", [P, KC, BLK], BF16)
        xin = sb("xin", [P, 2, H], F32)
        xq = sb("xq", [P, 2, H], BF16)
        h_hi = sb("h_hi", [P, NF, BLK], F16)
        h_lo = sb("h_lo", [P, NF, BLK], F16)
        t_hi = sb("t_hi", [P, NM, BLK], F16)
        t_lo = sb("t_lo", [P, NM, BLK], F16)
        half = sb("act_half", [P, RING, 512], F32)
        h32 = sb("h32", [P, 2, BLK], F32)
        t32 = sb("t32", [P, 2, BLK], F32)
        delta = sb("delta", [P, BLK], F32)
        idf = sb("ident_f32", [P, P], F32)
        idb = sb("ident_bf16", [P, P], BF16)
        sc = sb("scalars", [P, 3 + G], F32)
        lp = sb("local_point", [P, 1], F32)
        st6 = sb("st6", [P, 6], F32)
        unused = sb("unused", [P, 1], F32)
        mv = sb("mean_var", [P, TT, 2], F32)
        ve = sb("var_eps", [P, TT], F32)
        rs = sb("rstd", [P, TT], F32)
        neghalf = sb("neg_half", [P, 1], F32)
        xabs = sb("x_abs_sum", [P, TT], F32)
        beta = sb("beta", [P, TT], F32)
        beta_e = sb("beta_eps", [P, TT], F32)
        rbeta = sb("r_beta", [P, TT], F32)
        b2 = sb("beta_sq", [P, 1], F32)
        cB = sb("prod_scale", [P, 1], F32)
        cBa = sb("prod_scale_abs", [P, 1], F32)
        pmax = sb("prod_max", [P, 1], F32)
        gam = sb("gamma", [P, 1], F32)
        game = sb("gamma_eps", [P, 1], F32)
        rgam = sb("r_gamma", [P, 1], F32)
        qs = sb("q_scale", [P, 1], F32)
        od = sb("out_scale", [P, TT], F32)
        expo = sb("expo", [P, G], F32)
        ratio = sb("ratio", [P, G], F32)
        wabs = sb("w_abs_sum", [P, 3], F32)
        wtail = sb("w_abs_tail", [P, 1], F32)
        wtot = sb("w_abs_total", [P, 3], F32)
        wmean = sb("w_mean", [P, 3], F32)
        wmean_e = sb("w_mean_eps", [P, 3], F32)
        rw = sb("r_w_mean", [P, 3], F32)
        wsc = sb("w_scale", [P, 3], F32)

        bankA = [ctx.enter_context(nc.psum_tensor(f"pair_a{n}", [P, 512], F32)) for n in range(RING)]
        bankB = [ctx.enter_context(nc.psum_tensor(f"pair_b{n}", [P, 512], F32)) for n in range(RING)]
        tpX = ctx.enter_context(nc.psum_tensor("tp_x", [P, 512], F32))
        tpQ = ctx.enter_context(nc.psum_tensor("tp_q", [P, 1024], BF16))
        NQ1 = 8
        tpX_b = tpX[:, :].bitcast(BF16)


        got_x = [sem(f"got_x{s}") for s in range(2)]
        got_res = [sem(f"got_res{s}") for s in range(2)]
        stored = [sem(f"stored{s}") for s in range(2)]
        got_small = sem("got_small")
        got_ws = sem("got_ws")
        got_wf = [sem(f"got_wf{j}") for j in range(NF)]
        got_bit = [sem(f"got_bit{n}") for n in range(3)]
        got_poly = sem("got_poly")
        got_wd = sem("got_wd")
        const_ready = sem("const_ready")
        expo_ready = sem("expo_ready")
        ratio_ready = sem("ratio_ready")
        front_v = sem("front_v")
        rstd_ready = sem("rstd_ready")
        xabs_ready = sem("xabs_ready")
        x_tp = sem("x_transposed")
        xhi_ready = sem("xhi_ready")
        xlo_ready = sem("xlo_ready")
        xqT_ready = sem("xqT_ready")
        w_hi = sem("w_hi")
        w_lo = sem("w_lo")
        bit_abs = sem("bit_abs")
        down_sum = sem("down_sum")
        bit_tot = sem("bit_tot")
        bit_mean = sem("bit_mean")
        bit_round = sem("bit_round")
        bit_clip = sem("bit_clip")
        pair_ready = sem("pair_ready")
        pair_free = sem("pair_free")
        relu_ready = sem("relu_ready")
        half_ready = sem("half_ready")
        term_ready = sem("term_ready")
        keep_v = sem("keep_v")
        t_hi_ready = sem("t_hi_ready")
        t_lo_ready = sem("t_lo_ready")
        h_hi_ready = sem("h_hi_ready")
        h_lo_ready = sem("h_lo_ready")
        bit_v = sem("bit_v")
        q8_round = sem("q8_round")
        q8_tp = sem("q8_transposed")
        q8T_ready = sem("q8T_ready")
        out_v = sem("out_v")

        def w_unit(t, u, part, lo=0, n=512):
            return t[:, u, 512 * part + lo:512 * part + lo + n]

        def raw_unit(t, u, n=512):
            return t[:, u + 1, :].bitcast(F32)[:, 0:n]

        S_UNITS = [(WF, u, 512, P) for u in range(NS)]
        F_UNITS = [(WF, NS + u, KC * F_TILES[u // 2][1], P) for u in range(2 * NF)]
        D_UNIT_K = [P] * NM + [n for _, n in F_TILES]
        D_UNITS_L = [(WD, u, H, D_UNIT_K[u]) for u in range(D_UNITS)]
        UNITS = S_UNITS + F_UNITS + D_UNITS_L
        U_F, U_D = len(S_UNITS), len(S_UNITS) + len(F_UNITS)

        PREP = {
            4: [("sum", 0)], 5: [("mean", 0), ("round", 0)], 6: [("clip", 0), ("sum", 1)],
            7: [("mean", 1), ("round", 1)], 8: [("clip", 1)], 9: [("sum", 2)], 10: [("mean", 2), ("round", 2)],
            11: [("clip", 2)],
        }
        for j in range(2, NF):
            PREP[j - 1] = [("split", U_F + 2 * j), ("split", U_F + 2 * j + 1)] + PREP.get(j - 1, [])
        for u in range(D_UNITS):
            PREP.setdefault(FIRST_D - 1 - (D_UNITS - 1 - u) // 2, []).append(("split", U_D + u))

        def no_prep(i):
            pass

        def unit_wait(eng, n):
            if n < U_F:
                eng.wait_ge(got_ws, 16)
            elif n < U_D:
                eng.wait_ge(got_wf[(n - U_F) // 2], 16)
            elif n < U_D + NM:
                eng.wait_ge(got_poly, 16)
            else:
                eng.wait_ge(got_wd, 32)

        BITS = [
            (raw_bd, WBD[:, :, :].rearrange("p c h -> p (c h)"), NI * H, I * H),
            (raw_bg, WB[:, 0, :], KC * I, I * H),
            (raw_bu, WB[:, 1, :], KC * I, I * H),
        ]
        BD_MAIN = (NI - 1) * H
        BD_TAIL = I_CHUNKS[-1][1]
        BIT_SCAL = [2, 0, 1]

        def parts(m):
            if m == 0:
                return [(slice(0, P), slice(0, BD_MAIN)), (slice(0, BD_TAIL), slice(BD_MAIN, NI * H))]
            return [(slice(0, P), slice(0, KC * I))]

        block = ctx.enter_context(nc.Block())

        @block.sync
        def _(sp):
            x_t = x.rearrange("(n p) h -> n p h", p=P)
            out_t = out.rearrange("(n p) h -> n p h", p=P)

            def load_x(n, s):
                sp.dma_start(xin[:, s, :], x_t[n, :, :]).then_inc(got_x[s], 16)

            def load_res(n, s):
                sp.dma_start(res[:, s, :], x_t[n, :, :]).then_inc(got_res[s], 16)

            load_x(0, 0)
            load_x(1, 1)
            sp.dma_start(idf[:, :], ident).then_inc(got_small, 16)
            sp.dma_start(sc[:, :], scal.partition_broadcast(P)).then_inc(got_small, 16)
            sp.dma_start(lp[:, :], local_point).then_inc(got_small, 16)
            sp.dma_start(WF[:, 1:NS + 1, :].rearrange("p u c -> p (u c)").bitcast(F32), w_s).then_inc(got_ws, 16)
            for j in range(2):
                sp.dma_start(WF[:, NS + 2 * j + 1:NS + 2 * j + 3, :].rearrange("p u c -> p (u c)").bitcast(F32),
                             w_f[:, 1024 * j:1024 * (j + 1)]).then_inc(got_wf[j], 16)
            for n in range(2, TT):
                sp.wait_ge(x_tp, n - 1)
                load_x(n, n % 2)
            for j in range(2, NF - 1):
                sp.dma_start(WF[:, NS + 2 * j + 1:NS + 2 * j + 3, :].rearrange("p u c -> p (u c)").bitcast(F32),
                             w_f[:, 1024 * j:1024 * (j + 1)]).then_inc(got_wf[j], 16)
            tail = KC * F_TILES[-1][1]
            sp.dma_start(WF[:, NS + 2 * NF - 1:NS + 2 * NF + 1, :].bitcast(F32)[:, :, 0:tail],
                         w_f_tail.rearrange("p (u c) -> p u c", u=2)).then_inc(got_wf[NF - 1], 16)
            sp.dma_start(raw_bd[:, 0:BD_MAIN].rearrange("p (c h) -> p c h", h=H),
                         w_bd[0:(NI - 1) * P, :].rearrange("(c p) h -> p c h", p=P)).then_inc(got_bit[0], 16)
            sp.dma_start(raw_bd[0:BD_TAIL, BD_MAIN:NI * H], w_bd[(NI - 1) * P:I, :]).then_inc(got_bit[0], 16)
            sp.dma_start(raw_bg.rearrange("p (k i) -> p k i", k=KC),
                         w_bg.rearrange("(k p) i -> p k i", p=P)).then_inc(got_bit[1], 16)
            sp.wait_ge(bit_clip, 2)
            sp.dma_start(raw_bu.rearrange("p (k i) -> p k i", k=KC),
                         w_bu.rearrange("(k p) i -> p k i", p=P)).then_inc(got_bit[2], 16)
            sp.wait_ge(bit_clip, 4)
            sp.dma_start(WD[:, 1:NM + 1, :].rearrange("p u c -> p (u c)").bitcast(F32), w_poly).then_inc(got_poly, 16)
            sp.dma_start(WD[:, NM + 1:D_UNITS, :].bitcast(F32),
                         w_down[0:(NF - 1) * P, :].rearrange("(c p) h -> p c h", p=P)).then_inc(got_wd, 16)
            sp.dma_start(WD[0:D_UNIT_K[-1], D_UNITS, :].bitcast(F32), w_down[(NF - 1) * P:F, :]).then_inc(got_wd, 16)
            sp.wait_ge(bit_clip, 6)
            load_res(0, 0)
            load_res(1, 1)

            def down(b, front):
                for t in range(TT):
                    n = b * TT + t
                    if front:
                        sp.wait_ge(x_tp, n + 3)
                        load_x(n + TT, t % 2)
                    sp.wait_ge(pair_free, PER_BLOCK * b + FIRST_D + t + 1)
                    sp.dma_start(out_t[n, :, :], res[:, t % 2, :]).then_inc(stored[t % 2], 16)
                    if front or t < TT - 2:
                        sp.wait_ge(stored[t % 2], 16 * (TT // 2) * b + 16 * (t // 2 + 1))
                        load_res(n + 2, t % 2)

            with sp.Fori(0, NB - 1) as b:
                down(b, True)
            down(NB - 1, False)
            for s in range(2):
                sp.wait_ge(stored[s], TOK // P // 2 * 16)

        @block.gpsimd
        def _(pool):
            pool.wait_ge(const_ready, 1)

            def rstd(n, t):
                pool.wait_ge(front_v, FRONT * n + 3)
                nc.gpsimd.tensor_tensor(rs[:, t:t + 1], ve[:, t:t + 1], neghalf[:, :], ALU.pow).then_inc(rstd_ready, 1)

            for t in range(TT):
                rstd(t, t)
            for m in range(3):
                if m == 0:
                    pool.wait_ge(down_sum, 1)
                else:
                    pool.wait_ge(bit_abs, m + 1)
                nc.gpsimd.partition_all_reduce(wtot[:, m:m + 1], wabs[:, m:m + 1], P, RADD).then_inc(bit_tot, 1)
            with pool.Fori(0, NB - 1) as b:
                for t in range(TT):
                    rstd((b + 1) * TT + t, t)

        @block.scalar
        def _(act):
            def front_abs(n, t):
                act.wait_ge(front_v, FRONT * n + XN)
                if not (isinstance(n, int) and n < 2):
                    act.wait_ge(x_tp, n - 1)
                nc.scalar.activation(xq[:, t % 2, :], xin[:, t % 2, :], ACT.Abs,
                                     accum_out=xabs[:, t:t + 1]).then_inc(xabs_ready, 1)

            def front_evac(n, t):
                act.wait_ge(x_tp, n + 1)
                nc.scalar.copy(xT_hi[:, :, P * t:P * (t + 1)],
                               tpX[:, :].rearrange("p (k t) -> p k t", k=KC)).then_inc(xhi_ready, 1)
                nc.scalar.copy(xqT[:, :, P * t:P * (t + 1)],
                               tpQ[:, 0:KC * P].rearrange("p (k t) -> p k t", k=KC)).then_inc(xqT_ready, 1)

            def split_hi(n):
                tensor, u, cols, rows = UNITS[n]
                unit_wait(act, n)
                if n not in (0, U_D):
                    act.wait_ge(w_lo, n)
                nc.scalar.mul(w_unit(tensor, u, 0, 0, cols)[0:rows, :], raw_unit(tensor, u, cols)[0:rows, :],
                              WS).then_inc(w_hi, 1)

            def bit_sum(m):
                raw, dst, _, _ = BITS[m]
                act.wait_ge(got_bit[m], 32 if m == 0 else 16)
                for k, (rows, cols) in enumerate(parts(m)):
                    to = wabs[:, m:m + 1] if k == 0 else wtail[rows, :]
                    last = nc.scalar.activation(dst[rows, cols], raw[rows, cols], ACT.Abs, accum_out=to)
                last.then_inc(bit_abs, 1)

            def bit_rounding(m):
                raw, _, _, _ = BITS[m]
                act.wait_ge(bit_mean, 3 * (m + 1))
                for rows, cols in parts(m):
                    last = nc.scalar.activation(raw[rows, cols], raw[rows, cols], ACT.Copy, bias=MAGIC,
                                                scale=rw[rows, m:m + 1])
                last.then_inc(bit_round, 1)

            def terms(b):
                for m in range(NM):
                    act.wait_ge(term_ready, NM * b + m + 1)
                    nc.scalar.copy(t_hi[:, m, :], t32[:, m % 2, :]).then_inc(t_hi_ready, 1)

            def f_gate(b, j, i):
                rows = F_TILES[j][1]
                act.wait_ge(pair_ready, PER_BLOCK * b + i + 1)
                nc.scalar.activation(half[0:rows, i % RING, 0:BLK], bankA[i % RING][0:rows, 0:BLK], ACT.Silu,
                                     scale=1.0 / WS).then_inc(half_ready, 1)

            def f_hi(b, j, i):
                rows = F_TILES[j][1]
                act.wait_ge(pair_free, PER_BLOCK * b + i + 1)
                nc.scalar.copy(h_hi[0:rows, j, :], h32[0:rows, j % 2, :]).then_inc(h_hi_ready, 1)

            def b_gate(b, n, i):
                c = n % NC
                cols = B_COLS[c][1]
                act.wait_ge(pair_ready, PER_BLOCK * b + i + 1)
                nc.scalar.activation(half[:, i % RING, 0:cols], bankA[i % RING][:, 0:cols], ACT.Relu,
                                     scale=wsc[:, 1:2]).then_inc(relu_ready, 1)
                act.wait_ge(relu_ready, TT * NC * b + n + 1)
                nc.scalar.activation(half[:, i % RING, 0:cols], half[:, i % RING, 0:cols],
                                     ACT.Square).then_inc(half_ready, 1)

            def b_round(b, t):
                act.wait_ge(bit_v, BIT * (b * TT + t) + BIT_SCALE)
                nc.scalar.activation(prod, prod, ACT.Copy, bias=MAGIC, scale=qs[:, 0:1]).then_inc(q8_round, 1)

            def up(b, order, prep):
                due = None
                for i, (kind, n) in enumerate(order):
                    prep(i)
                    if kind == "S":
                        terms(b)
                    elif kind == "F":
                        f_gate(b, n, i)
                        if due is not None:
                            b_round(b, due)
                            due = None
                        f_hi(b, n, i)
                    else:
                        if due is not None:
                            b_round(b, due)
                            due = None
                        b_gate(b, n, i)
                        if n % NC == NC - 1:
                            due = n // NC
                b_round(b, due)

            def down(b, front):
                for t in range(TT):
                    n = b * TT + t
                    act.wait_ge(q8_tp, n + 1)
                    nc.scalar.copy(q8T[:, 0:NQ1, :], tpX_b.rearrange("p (c t) -> p c t", t=P))
                    nc.scalar.copy(q8T[:, NQ1:NI - 1, :],
                                   tpQ[:, 0:(NI - 1 - NQ1) * P].rearrange("p (c t) -> p c t", t=P))
                    nc.scalar.copy(q8T[0:BD_TAIL, NI - 1, :],
                                   tpQ[0:BD_TAIL, (NI - 1 - NQ1) * P:(NI - NQ1) * P]).then_inc(q8T_ready, 1)
                    if front:
                        front_abs(n + TT, t)
                        front_evac(n + TT, t)

            act.wait_ge(expo_ready, 2)
            nc.scalar.activation(ratio[:, :], expo[:, :], ACT.Exp).then_inc(ratio_ready, 1)
            for n in range(U_F):
                split_hi(n)
            for t in range(TT):
                front_abs(t, t)
                front_evac(t, t)
            for n in range(U_F, U_F + 4):
                split_hi(n)

            def prep(i):
                for what, n in PREP.get(i, []):
                    if what == "split":
                        split_hi(n)
                    elif what == "sum":
                        bit_sum(n)
                    elif what == "round":
                        bit_rounding(n)

            up(0, FIRST, prep)
            with act.Fori(0, NB - 1) as b:
                down(b, True)
                up(b + 1, STEADY, no_prep)
            down(NB - 1, False)

        @block.vector
        def _(dve):
            def front(b, t):
                n = b * TT + t

                def step(k, ins):
                    ins.then_inc(front_v, 1)
                    dve.wait_ge(front_v, FRONT * n + k)

                one = slice(t, t + 1)
                xt = xin[:, t % 2, :]
                tmp = t32[:, t % 2, :]
                dve.wait_ge(got_x[t % 2], 16 * (TT // 2) * b + 16 * (t // 2 + 1))
                step(1, nc.vector.bn_stats(st6[:, :], xt))
                nc.vector.memset(unused[:, :], 0.0)
                step(2, nc.vector.bn_aggr(mv[:, t, :], st6[:, :]))
                nc.vector.tensor_scalar_add(ve[:, one], mv[:, t, 1:2], LN_EPS).then_inc(front_v, 1)
                dve.wait_ge(rstd_ready, n + 1)
                nc.vector.tensor_scalar(xt, xt, mv[:, t, 0:1], rs[:, one], ALU.subtract,
                                        ALU.mult).then_inc(front_v, 1)
                dve.wait_ge(xabs_ready, n + 1)
                nc.vector.tensor_scalar_mul(beta[:, one], xabs[:, one], 1.0 / H)
                step(5, nc.vector.tensor_scalar(beta_e[:, one], xabs[:, one], 1.0 / H, Q_EPS, ALU.mult, ALU.add))
                step(6, nc.vector.reciprocal(rbeta[:, one], beta_e[:, one]))
                step(7, nc.vector.tensor_scalar(tmp, xt, rbeta[:, one], SQRT7, ALU.mult, ALU.mult))
                step(8, nc.vector.tensor_scalar(tmp, tmp, MAGIC, MAGIC - 8.0, ALU.add, ALU.max))
                nc.vector.tensor_scalar(xq[:, t % 2, :], tmp, MAGIC + 7.0, MAGIC, ALU.min,
                                        ALU.subtract).then_inc(front_v, 1)

            def front_evac(n, t):
                dve.wait_ge(xhi_ready, n + 1)
                part = xT_hi[:, :, P * t:P * (t + 1)]
                nc.vector.tensor_tensor(xT_lo[:, :, P * t:P * (t + 1)],
                                        tpX[:, :].rearrange("p (k t) -> p k t", k=KC), part,
                                        ALU.subtract).then_inc(xlo_ready, 1)

            def split_lo(n):
                tensor, u, cols, rows = UNITS[n]
                dve.wait_ge(w_hi, n + 1)
                nc.vector.scalar_tensor_tensor(w_unit(tensor, u, 1, 0, cols)[0:rows, :],
                                               raw_unit(tensor, u, cols)[0:rows, :], WS,
                                               w_unit(tensor, u, 0, 0, cols)[0:rows, :],
                                               ALU.mult, ALU.subtract).then_inc(w_lo, 1)

            def down_whole():
                dve.wait_ge(bit_abs, 1)
                nc.vector.tensor_tensor(wabs[0:BD_TAIL, 0:1], wabs[0:BD_TAIL, 0:1], wtail[0:BD_TAIL, :],
                                        ALU.add).then_inc(down_sum, 1)

            def bit_means(m):
                one = slice(m, m + 1)
                count = BITS[m][3]
                dve.wait_ge(bit_tot, m + 1)
                nc.vector.tensor_scalar_mul(wmean[:, one], wtot[:, one], 1.0 / count).then_inc(bit_mean, 1)
                nc.vector.tensor_scalar(wmean_e[:, one], wtot[:, one], 1.0 / count, Q_EPS, ALU.mult,
                                        ALU.add).then_inc(bit_mean, 1)
                dve.wait_ge(bit_mean, 3 * m + 2)
                nc.vector.tensor_tensor(wsc[:, one], wmean[:, one], sc[:, BIT_SCAL[m]:BIT_SCAL[m] + 1], ALU.mult)
                nc.vector.reciprocal(rw[:, one], wmean_e[:, one]).then_inc(bit_mean, 1)

            def bit_clipping(m):
                raw, dst, _, _ = BITS[m]
                dve.wait_ge(bit_round, m + 1)
                for rows, cols in parts(m):
                    last = nc.vector.tensor_scalar(raw[rows, cols], raw[rows, cols], MAGIC - 1.0, MAGIC + 1.0,
                                                   ALU.max, ALU.min)
                last.then_inc(bit_clip, 1)
                dve.wait_ge(bit_clip, 2 * m + 1)
                for rows, cols in parts(m):
                    last = nc.vector.tensor_scalar_sub(dst[rows, cols], raw[rows, cols], MAGIC)
                last.then_inc(bit_clip, 1)

            def terms(b, i):
                a, g = bankA[i % RING], bankB[i % RING]
                free = PER_BLOCK * b + i + 1

                def lo(m):
                    dve.wait_ge(t_hi_ready, NM * b + m + 1)
                    nc.vector.tensor_tensor(t_lo[:, m, :], t32[:, m % 2, :], t_hi[:, m, :],
                                            ALU.subtract).then_inc(t_lo_ready, 1)

                dve.wait_ge(pair_ready, free)
                nc.vector.tensor_scalar_mul(t32[:, 0, :], a[:, :], 1.0 / WS).then_inc(term_ready, 1)
                nc.vector.tensor_scalar(delta[:, :], g[:, :], 1.0 / WS, lp[:, 0:1], ALU.mult,
                                        ALU.subtract).then_inc(pair_free, 1)
                dve.wait_ge(pair_free, free)
                for m in range(1, NM):
                    if m == 5:
                        dve.wait_ge(term_ready, NM * b + m)
                        nc.vector.scalar_tensor_tensor(delta[:, :], delta[:, :], THD, delta[:, :], ALU.is_le,
                                                       ALU.mult).then_inc(keep_v, 1)
                        dve.wait_ge(keep_v, 2 * b + 1)
                        nc.vector.scalar_tensor_tensor(delta[:, :], delta[:, :], -THD, delta[:, :], ALU.is_ge,
                                                       ALU.mult).then_inc(keep_v, 1)
                        dve.wait_ge(keep_v, 2 * b + 2)
                    dve.wait_ge(term_ready, NM * b + m)
                    if m >= 2:
                        dve.wait_ge(t_lo_ready, NM * b + m - 1)
                    nc.vector.scalar_tensor_tensor(t32[:, m % 2, :], delta[:, :], ratio[:, m - 1:m],
                                                   t32[:, (m - 1) % 2, :], ALU.mult,
                                                   ALU.mult).then_inc(term_ready, 1)
                    lo(m - 1)
                lo(NM - 1)

            def f_product(b, j, i):
                rows = F_TILES[j][1]
                dve.wait_ge(half_ready, half_count(b, i))
                if j >= 2:
                    dve.wait_ge(h_lo_ready, NF * b + j - 1)
                nc.vector.scalar_tensor_tensor(h32[0:rows, j % 2, :], bankB[i % RING][0:rows, :], 1.0 / WS,
                                               half[0:rows, i % RING, :], ALU.mult, ALU.mult).then_inc(pair_free, 1)

            def half_count(b, i):
                return (NF + TT * NC) * b + i

            def f_lo(b, j):
                rows = F_TILES[j][1]
                dve.wait_ge(h_hi_ready, NF * b + j + 1)
                nc.vector.tensor_tensor(h_lo[0:rows, j, :], h32[0:rows, j % 2, :], h_hi[0:rows, j, :],
                                        ALU.subtract).then_inc(h_lo_ready, 1)

            def b_product(b, n, i):
                o, cols = B_COLS[n % NC]
                dve.wait_ge(half_ready, half_count(b, i))
                nc.vector.tensor_tensor(prod[:, o:o + cols], bankB[i % RING][:, 0:cols],
                                        half[:, i % RING, 0:cols], ALU.mult).then_inc(pair_free, 1)
                if n % NC == NC - 1:
                    dve.wait_ge(pair_free, PER_BLOCK * b + i + 1)
                    b_scale(b, n // NC)

            def b_scale(b, t):
                def step(k, ins):
                    ins.then_inc(bit_v, 1)
                    dve.wait_ge(bit_v, BIT * (b * TT + t) + k)

                bt = beta[:, t:t + 1]
                nc.vector.tensor_tensor(b2[:, :], bt, bt, ALU.mult).then_inc(bit_v, 1)
                step(2, nc.vector.tensor_reduce(pmax[:, :], prod, AX_X, ALU.max, apply_absolute_value=True))
                step(3, nc.vector.scalar_tensor_tensor(cB[:, :], bt, wsc[:, 2:3], b2[:, :], ALU.mult, ALU.mult))
                step(4, nc.vector.scalar_tensor_tensor(cBa[:, :], cB[:, :], -1.0, cB[:, :], ALU.mult, ALU.max))
                nc.vector.tensor_tensor(gam[:, :], cBa[:, :], pmax[:, :], ALU.mult)
                step(5, nc.vector.tensor_scalar(game[:, :], cBa[:, :], pmax[:, :], Q_EPS, ALU.mult, ALU.add))
                nc.vector.tensor_scalar(od[:, t:t + 1], gam[:, :], 1.0 / 127.0, wsc[:, 0:1], ALU.mult, ALU.mult)
                step(6, nc.vector.reciprocal(rgam[:, :], game[:, :]))
                step(7, nc.vector.tensor_scalar(qs[:, :], rgam[:, :], 127.0, cB[:, :], ALU.mult, ALU.mult))

            def b_store(b, t):
                base = BIT * (b * TT + t)
                dve.wait_ge(q8_round, b * TT + t + 1)
                nc.vector.tensor_scalar(prod, prod, MAGIC - 128.0, MAGIC + 127.0, ALU.max,
                                        ALU.min).then_inc(bit_v, 1)
                dve.wait_ge(bit_v, base + 8)
                nc.vector.tensor_scalar_sub(q8[:, t, :], prod, MAGIC).then_inc(bit_v, 1)

            def up(b, order, prep):
                for i, (kind, n) in enumerate(order):
                    prep(i)
                    if kind == "S":
                        terms(b, i)
                    elif kind == "F":
                        f_product(b, n, i)
                        if n > 0:
                            f_lo(b, n - 1)
                    else:
                        if n % NC == 0 and n > 0:
                            b_store(b, n // NC - 1)
                            dve.wait_ge(bit_v, BIT * (b * TT + n // NC))
                        b_product(b, n, i)
                    if (kind, n) == ("F", NF - 1):
                        f_lo(b, n)
                b_store(b, TT - 1)

            def down(b, is_front):
                for t in range(TT):
                    n = b * TT + t
                    i = FIRST_D + t
                    if is_front:
                        front(b + 1, t)
                        front_evac(n + TT, t)
                    dve.wait_ge(got_res[t % 2], 16 * (TT // 2) * b + 16 * (t // 2 + 1))
                    dve.wait_ge(pair_ready, PER_BLOCK * b + i + 1)
                    nc.vector.scalar_tensor_tensor(res[:, t % 2, :], bankA[i % RING][:, :], 1.0 / WS,
                                                   res[:, t % 2, :], ALU.mult, ALU.add).then_inc(out_v, 1)
                    dve.wait_ge(out_v, n + 1)
                    nc.vector.scalar_tensor_tensor(res[:, t % 2, :], bankB[i % RING][:, :], od[:, t:t + 1],
                                                   res[:, t % 2, :], ALU.mult, ALU.add).then_inc(pair_free, 1)

            nc.vector.memset(neghalf[:, :], -0.5).then_inc(const_ready, 1)
            dve.wait_ge(got_small, 48)
            nc.vector.tensor_scalar_mul(expo[:, 0:1], sc[:, 3:4], -1.0).then_inc(expo_ready, 1)
            nc.vector.tensor_tensor(expo[:, 1:G], sc[:, 3:2 + G], sc[:, 4:3 + G], ALU.subtract).then_inc(expo_ready, 1)
            nc.vector.tensor_copy(idb[:, :], idf[:, :]).then_inc(const_ready, 1)
            for n in range(U_F):
                split_lo(n)
            for t in range(TT):
                front(0, t)
                front_evac(t, t)
            for n in range(U_F, U_F + 4):
                split_lo(n)
            dve.wait_ge(ratio_ready, 1)

            def prep(i):
                for what, n in PREP.get(i, []):
                    if what == "split":
                        split_lo(n)
                    elif what == "sum" and n == 0:
                        down_whole()
                    elif what == "mean":
                        bit_means(n)
                    elif what == "clip":
                        bit_clipping(n)

            up(0, FIRST, prep)
            with dve.Fori(0, NB - 1) as b:
                down(b, True)
                up(b + 1, STEADY, no_prep)
            down(NB - 1, False)

        @block.tensor
        def _(pe):
            def split_product(bank, w, xx, ks, last_of_all=True, first=True):
                for k in ks:
                    for wp, xp in ((0, 0), (0, 1), (1, 0)):
                        ins = nc.tensor.matmul(bank, w(wp, k), xx(xp, k),
                                               start=(first and k == ks[0] and (wp, xp) == (0, 0)),
                                               stop=(last_of_all and k == ks[-1] and wp == 1))
                return ins

            def xT(part, k):
                return (xT_lo if part else xT_hi)[:, k, :]

            def free(b, i):
                if not (isinstance(b, int) and PER_BLOCK * b + i < RING):
                    pe.wait_ge(pair_free, PER_BLOCK * b + i - RING + 1)

            def front_transposes(b, t):
                n = b * TT + t
                pe.wait_ge(front_v, FRONT * n + XQ)
                if not (isinstance(n, int) and n == 0):
                    pe.wait_ge(xlo_ready, n)
                    pe.wait_ge(xqT_ready, n)
                for k in range(KC):
                    nc.tensor.transpose(tpX[:, P * k:P * (k + 1)], xin[:, t % 2, P * k:P * (k + 1)], idf[:, :])
                for k in range(KC):
                    ins = nc.tensor.transpose(tpQ[:, P * k:P * (k + 1)], xq[:, t % 2, P * k:P * (k + 1)], idb[:, :])
                ins.then_inc(x_tp, 1)

            def s_pair(b, i):
                free(b, i)
                pe.wait_ge(xlo_ready, TT * (b + 1))
                pe.wait_ge(w_lo, U_F)
                split_product(bankA[i % RING][:, :], lambda q, k: w_unit(WF, 0, q, P * k, P), xT, range(KC))
                split_product(bankB[i % RING][:, :], lambda q, k: w_unit(WF, 1, q, P * k, P), xT,
                              range(KC)).then_inc(pair_ready, 1)

            def f_pair(b, j, i, first_use):
                n = F_TILES[j][1]
                free(b, i)
                if first_use:
                    pe.wait_ge(w_lo, U_F + 2 * j + 2)
                split_product(bankA[i % RING][0:n, :], lambda q, k: w_unit(WF, NS + 2 * j, q, n * k, n), xT, range(KC))
                split_product(bankB[i % RING][0:n, :], lambda q, k: w_unit(WF, NS + 2 * j + 1, q, n * k, n), xT,
                              range(KC)).then_inc(pair_ready, 1)

            def b_pair(b, m, i, first_use):
                t = m // NC
                o, n = B_COLS[m % NC]
                free(b, i)
                if m == 0:
                    pe.wait_ge(xqT_ready, TT * (b + 1))
                    if first_use:
                        pe.wait_ge(bit_clip, 6)
                for side, bank in ((0, bankA[i % RING]), (1, bankB[i % RING])):
                    for k in range(KC):
                        ins = nc.tensor.matmul(bank[:, 0:n], xqT[:, k, P * t:P * (t + 1)],
                                               WB[:, side, I * k + o:I * k + o + n],
                                               start=(k == 0), stop=(k == KC - 1))
                ins.then_inc(pair_ready, 1)

            def up(b, order, first_use):
                for i, (kind, n) in enumerate(order):
                    if kind == "S":
                        s_pair(b, i)
                    elif kind == "F":
                        f_pair(b, n, i, first_use)
                    else:
                        b_pair(b, n, i, first_use)

            def down(b, front):
                for t in range(TT):
                    n = b * TT + t
                    i = FIRST_D + t
                    pe.wait_ge(bit_v, BIT * n + BIT)
                    if front:
                        pe.wait_ge(xlo_ready, n + TT)
                        pe.wait_ge(xqT_ready, n + TT)
                    for c, (o, kk) in enumerate(I_CHUNKS):
                        to = tpX_b[0:kk, P * c:P * (c + 1)] if c < NQ1 else tpQ[0:kk, P * (c - NQ1):P * (c - NQ1 + 1)]
                        ins = nc.tensor.transpose(to, q8[:, t, o:o + kk], idb[:, :])
                    ins.then_inc(q8_tp, 1)
                    free(b, i)
                    tok = slice(P * t, P * (t + 1))

                    def act_part(q, u):
                        if u < NM:
                            return (t_lo if q else t_hi)[:, u, tok]
                        kk = F_TILES[u - NM][1]
                        return (h_lo if q else h_hi)[0:kk, u - NM, tok]

                    def w_part(q, u):
                        return w_unit(WD, u, q)[0:D_UNIT_K[u], :]

                    if t == 0:
                        pe.wait_ge(t_lo_ready, NM * (b + 1))
                        pe.wait_ge(w_lo, U_D + NM)
                    bank = bankA[i % RING][:, :]
                    split_product(bank, act_part, w_part, range(NM), last_of_all=False)
                    if t == 0:
                        pe.wait_ge(h_lo_ready, NF * (b + 1))
                        pe.wait_ge(w_lo, U_D + D_UNITS)
                    split_product(bank, act_part, w_part, range(NM, D_UNITS), first=False)
                    pe.wait_ge(q8T_ready, n + 1)
                    if front:
                        front_transposes(b + 1, t)
                    for c, (o, kk) in enumerate(I_CHUNKS):
                        ins = nc.tensor.matmul(bankB[i % RING][:, :], q8T[0:kk, c, :], WBD[0:kk, c, :],
                                               start=(c == 0), stop=(c == NI - 1))
                    ins.then_inc(pair_ready, 1)

            pe.wait_ge(const_ready, 2)
            for t in range(TT):
                front_transposes(0, t)
            up(0, FIRST, True)
            with pe.Fori(0, NB - 1) as b:
                down(b, True)
                up(b + 1, STEADY, False)
            down(NB - 1, False)


def kernel(**inputs):
    import numpy as np
    import concourse.bacc as bacc
    from concourse.bass_utils import run_bass_kernel_spmd

    def get(name):
        return np.asarray(inputs["L0_" + name])

    x = get("attn_hidden_states")
    B, T, H = x.shape
    KC = H // P

    def chunked(w):
        return w.T.reshape(KC, P, w.shape[0]).transpose(1, 0, 2)

    def flat(*parts):
        return np.ascontiguousarray(np.concatenate([a.reshape(a.shape[0], -1) for a in parts], axis=1))

    gate, up = chunked(get("attn_ffn_gate_w")), chunked(get("attn_ffn_up_w"))
    F = gate.shape[2]
    whole = F // P * P
    fuse = get("attn_fuse_weight")
    arrays = {
        "x": np.ascontiguousarray(x.reshape(B * T, H)),
        "w_s": flat(chunked(get("attn_up_w")), chunked(get("attn_gate_w"))),
        "w_f": flat(*[w[:, :, o:o + P] for o in range(0, whole, P) for w in (gate, up)]),
        "w_f_tail": flat(gate[:, :, whole:], up[:, :, whole:]),
        "w_poly": flat(get("attn_local_approx_output").T, fuse.transpose(1, 2, 0)),
        "w_down": np.ascontiguousarray(get("attn_ffn_down_w").T),
        "w_bg": np.ascontiguousarray(get("ffn_w_gate").T),
        "w_bu": np.ascontiguousarray(get("ffn_w_up").T),
        "w_bd": np.ascontiguousarray(get("ffn_w_down").T),
        "local_point": np.ascontiguousarray(get("attn_local_point").reshape(-1, 1)),
        "scal": np.concatenate([get("ffn_s_gate"), get("ffn_s_up"), get("ffn_s_down"),
                                get("attn_discount_factor")]),
        "ident": np.eye(P, dtype=np.float32),
    }
    nc = bacc.Bacc("TRN2", target_bir_lowering=False, num_devices=1)
    arrays = {"in_" + n: a for n, a in arrays.items()}
    args = [nc.dram_tensor(n, a.shape, mybir.dt.from_np(a.dtype), kind="ExternalInput").ap()
            for n, a in arrays.items()]
    args.append(nc.dram_tensor("y", (B * T, H), F32, kind="ExternalOutput").ap())
    bass_kernel(nc, *args)
    r = run_bass_kernel_spmd(nc, [arrays], core_ids=[0])
    return r.results[0]["y"].reshape(B, T, H)
```

```python
import concourse.bass as bass
from concourse import mybir
from concourse.alu_op_type import AluOpType as ALU
from contextlib import ExitStack

ACT = mybir.ActivationFunctionType
F32 = mybir.dt.float32
F16 = mybir.dt.float16
BF16 = mybir.dt.bfloat16
AX_X = mybir.AxisListType.X
RADD = bass.bass_isa.ReduceOp.add

P = 128
MAGIC = 12582912.0
LN_EPS = 1e-5
Q_EPS = 1e-5
SQRT7 = 7.0 ** 0.5
THD = 2.5
WS = 64.0
RING = 3


def spans(n, step):
    return [(o, min(step, n - o)) for o in range(0, n, step)]


def bass_kernel(nc, x, w_s, w_f, w_f_tail, w_poly, w_down, w_bg, w_bu, w_bd, local_point, scal, ident, out):
    TOK, H = x.shape
    S = local_point.shape[0]
    G = w_poly.shape[1] // H - 1
    F = w_down.shape[0]
    I = w_bg.shape[1]
    BLK = 512
    NB = TOK // BLK
    TT = BLK // P
    KC = H // P
    F_TILES = spans(F, P)
    NF = len(F_TILES)
    I_CHUNKS = spans(I, P)
    NI = len(I_CHUNKS)
    B_COLS = spans(I, 512)
    NC = len(B_COLS)
    NM = G + 1
    D_UNITS = NM + NF
    assert S == P and BLK <= 512 and H == 512 and G == 6

    PER_BLOCK = 1 + NF + TT * NC + TT
    assert PER_BLOCK % RING == 0
    FIRST_D = PER_BLOCK - TT
    STEADY = [("S", 0)]
    for n in range(max(NF, TT * NC)):
        STEADY += [("F", n)] * (n < NF) + [("B", n)] * (n < TT * NC)
    FIRST = [("S", 0)] + [("F", n) for n in range(NF - 3)]
    for n in range(3):
        FIRST += [("B", 2 * n), ("B", 2 * n + 1), ("F", NF - 3 + n)]
    FIRST += [("B", n) for n in range(6, TT * NC)]

    STATS = 3
    QUANT = 5
    BIT = 9
    BIT_SCALE = 7

    ctx = ExitStack()
    with ctx:
        def sb(name, shape, dt):
            return ctx.enter_context(nc.sbuf_tensor(name, shape, dt))

        def sem(name):
            return ctx.enter_context(nc.semaphore(name))

        PIECES = [KC, KC, 6]
        NPIECES = sum(PIECES)
        NS = 2
        WF = sb("w_sf_split", [P, NS + 2 * NF + 1, 1024], F16)
        WD = sb("w_d_split", [P, D_UNITS + 1, 1024], F16)
        WB = sb("w_bit", [P, 2, KC * I], BF16)
        WBD = sb("w_bit_down", [P, NI, H], BF16)
        REGION = sb("region", [P, KC * I + H], F32)
        o = 0
        prod = REGION[:, o:o + I]
        o += I
        q8 = REGION[:, o:o + TT * I // 2].bitcast(BF16).rearrange("p (t i) -> p t i", t=TT)
        o += TT * I // 2
        q8T = REGION[:, o:o + NI * P // 2].bitcast(BF16).rearrange("p (c t) -> p c t", c=NI)
        o += NI * P // 2
        res = REGION[:, o:o + 2 * H].rearrange("p (s h) -> p s h", s=2)
        assert KC * I + H >= o + 2 * H

        xT_hi = sb("xT_hi", [P, KC, BLK], F16)
        xT_lo = sb("xT_lo", [P, KC, BLK], F16)
        xqT = sb("xqT", [P, KC, BLK], BF16)
        xin = sb("xin", [P, 2, H], F32)
        xq = sb("xq", [P, 2, H], BF16)
        xq_words = xq[:, :, :].rearrange("p s h -> p (s h)").bitcast(F32)
        h_hi = sb("h_hi", [P, NF, BLK], F16)
        h_lo = sb("h_lo", [P, NF, BLK], F16)
        t_hi = sb("t_hi", [P, NM, BLK], F16)
        t_lo = sb("t_lo", [P, NM, BLK], F16)
        half = sb("act_half", [P, RING, 512], F32)
        h32 = sb("h32", [P, 2, BLK], F32)
        t32 = sb("t32", [P, 2, BLK], F32)
        delta = sb("delta", [P, BLK], F32)
        idf = sb("ident_f32", [P, P], F32)
        idb = sb("ident_bf16", [P, P], BF16)
        sc = sb("scalars", [P, 3 + G], F32)
        lp = sb("local_point", [P, 1], F32)
        st6 = sb("st6", [P, 6], F32)
        unused = sb("unused", [P, 1], F32)
        mv = sb("mean_var", [P, TT, 2], F32)
        ve = sb("var_eps", [P, TT], F32)
        rs = sb("rstd", [P, TT], F32)
        warm = sb("warm", [P, 1], F32)
        neghalf = sb("neg_half", [P, 1], F32)
        xabs = sb("x_abs_sum", [P, TT], F32)
        beta = sb("beta", [P, TT], F32)
        beta_e = sb("beta_eps", [P, TT], F32)
        rbeta = sb("r_beta", [P, TT], F32)
        b2 = sb("beta_sq", [P, 1], F32)
        cB = sb("prod_scale", [P, 1], F32)
        cBa = sb("prod_scale_abs", [P, 1], F32)
        pmax = sb("prod_max", [P, 1], F32)
        gam = sb("gamma", [P, 1], F32)
        game = sb("gamma_eps", [P, 1], F32)
        rgam = sb("r_gamma", [P, 1], F32)
        qs = sb("q_scale", [P, 1], F32)
        od = sb("out_scale", [P, TT], F32)
        expo = sb("expo", [P, G], F32)
        ratio = sb("ratio", [P, G], F32)
        wabs = sb("w_abs_sum", [P, NPIECES], F32)
        wtot = sb("w_abs_total", [P, NPIECES], F32)
        wsum = sb("w_abs_whole", [P, 3], F32)
        wmean = sb("w_mean", [P, 3], F32)
        wmean_e = sb("w_mean_eps", [P, 3], F32)
        rw = sb("r_w_mean", [P, 3], F32)
        wsc = sb("w_scale", [P, 3], F32)

        bankA = [ctx.enter_context(nc.psum_tensor(f"pair_a{n}", [P, 512], F32)) for n in range(RING)]
        bankB = [ctx.enter_context(nc.psum_tensor(f"pair_b{n}", [P, 512], F32)) for n in range(RING)]
        tpX = ctx.enter_context(nc.psum_tensor("tp_x", [P, 512], F32))
        tpQ = ctx.enter_context(nc.psum_tensor("tp_q", [P, 1024], BF16))
        NQ1 = 8
        tpX_b = tpX[:, :].bitcast(BF16)
        FIRST_X = [tpX, bankA[1], bankB[1], bankA[2]]
        FIRST_XQ = [tpQ[:, 0:H], tpQ[:, H:2 * H], tpX_b[:, 0:H], tpX_b[:, H:2 * H]]

        got_x = [sem(f"got_x{s}") for s in range(2)]
        got_first = [sem(f"got_first{s}") for s in range(2)]
        got_res = [sem(f"got_res{s}") for s in range(2)]
        stored = [sem(f"stored{s}") for s in range(2)]
        got_scalars = sem("got_scalars")
        got_lp = sem("got_local_point")
        got_ident = sem("got_ident")
        got_ws = sem("got_ws")
        got_wf = [sem(f"got_wf{j}") for j in range(NF)]
        got_bit = [[sem(f"got_bit{m}_{k}") for k in range(PIECES[m])] for m in range(3)]
        got_wd = [sem(f"got_wd{n}") for n in range(3)]
        const_ready = sem("const_ready")
        idb_ready = sem("idb_ready")
        expo_ready = sem("expo_ready")
        ratio_ready = sem("ratio_ready")
        stats_v = sem("stats_v")
        xn_ready = sem("xn_ready")
        quant_v = sem("quant_v")
        rstd_ready = sem("rstd_ready")
        xabs_ready = sem("xabs_ready")
        x_tp = sem("x_transposed")
        xq_tp = sem("xq_transposed")
        xhi_ready = sem("xhi_ready")
        xlo_ready = sem("xlo_ready")
        xqT_ready = sem("xqT_ready")
        w_hi = sem("w_hi")
        w_lo = sem("w_lo")
        wd_hi = sem("wd_hi")
        wd_scaled = sem("wd_scaled")
        wd_lo = sem("wd_lo")
        tail_zero = sem("tail_zero")
        bit_abs = sem("bit_abs")
        bit_tot = sem("bit_tot")
        bit_mean = sem("bit_mean")
        bit_round = [sem(f"bit_round{m}") for m in range(3)]
        bit_clip = sem("bit_clip")
        pair_ready = sem("pair_ready")
        pair_free = sem("pair_free")
        relu_ready = sem("relu_ready")
        half_ready = sem("half_ready")
        term_ready = sem("term_ready")
        keep_v = sem("keep_v")
        t_hi_ready = sem("t_hi_ready")
        t_lo_ready = sem("t_lo_ready")
        h_hi_ready = sem("h_hi_ready")
        h_lo_ready = sem("h_lo_ready")
        bit_v = sem("bit_v")
        q8_round = sem("q8_round")
        q8_tp = sem("q8_transposed")
        q8T_ready = sem("q8T_ready")
        out_v = sem("out_v")

        def x_buffer(b, t):
            if isinstance(b, int) and b == 0 and t >= 2:
                return h32[:, t - 2, :]
            return xin[:, t % 2, :]

        def xq_buffer(b, t):
            if isinstance(b, int) and b == 0 and t >= 2:
                return h_lo[:, t, :].bitcast(BF16)
            return xq[:, t % 2, :]

        def w_unit(t, u, part, lo=0, n=512):
            return t[:, u, 512 * part + lo:512 * part + lo + n]

        def raw_unit(t, u, n=512):
            return t[:, u + 1, :].bitcast(F32)[:, 0:n]

        S_UNITS = [(WF, u, 512, P) for u in range(NS)]
        F_UNITS = [(WF, NS + u, KC * F_TILES[u // 2][1], P) for u in range(2 * NF)]
        UNITS = S_UNITS + F_UNITS
        U_F = NS
        D_UNIT_K = [P] * NM + [n for _, n in F_TILES]
        D_EARLY = 10

        def chunk_rows(c):
            return I_CHUNKS[c][1]

        WD_words = WD[:, :, :].rearrange("p u c -> p (u c)").bitcast(F32)
        WBD_cols = WBD[:, :, :].rearrange("p c h -> p (c h)")
        BITS = [
            [(WD_words[:, I * k:I * (k + 1)], WB[:, 0, I * k:I * (k + 1)], P) for k in range(KC)],
            [(REGION[:, I * k:I * (k + 1)], WB[:, 1, I * k:I * (k + 1)], P) for k in range(KC)],
            [],
        ]
        FREE = (D_EARLY + 1) * H
        assert KC * I <= FREE
        DOWN_CHUNKS = [(0, 3), (3, 5), (5, 7), (7, 9), (9, 10), (10, 11)]
        assert len(DOWN_CHUNKS) == PIECES[2] and DOWN_CHUNKS[-1][1] == NI and D_UNITS + 1 - D_EARLY - 1 == 7
        for c0, c1 in DOWN_CHUNKS:
            if c1 <= 7:
                raw = WD_words[:, FREE + H * c0:FREE + H * c1]
            elif c1 <= 9:
                raw = xin[:, :, :].rearrange("p s h -> p (s h)")
            elif c1 <= 10:
                raw = xq_words
            else:
                raw = REGION[0:chunk_rows(c0), KC * I:KC * I + H]
            BITS[2].append((raw, WBD_cols[0:chunk_rows(c0), H * c0:H * c1], chunk_rows(c0)))
        BIT_BASE = [0, PIECES[0], PIECES[0] + PIECES[1]]
        BIT_MEANS = 4
        BIT_SCAL = [0, 1, 2]

        PREP = {}

        def plan(i, *what):
            PREP[i] = PREP.get(i, []) + list(what)

        GATE, UP, DOWN = 0, 1, 2
        TERM_PREP = {1: [("split", U_F + 2)], 2: [("split", U_F + 3)], 3: [("sum", GATE, 0)],
                     4: [("split", U_F + 4)], 5: [("sum", GATE, 1)], 6: [("split", U_F + 5)]}
        plan(1, ("split", U_F + 6), ("sum", GATE, 2), ("split", U_F + 7), ("sum", GATE, 3))
        plan(2, ("xq", 0), ("split", U_F + 8), ("xq", 1), ("mean", GATE), ("split", U_F + 9), ("xq", 2), ("xq", 3),
             ("round", GATE, 0), ("round", GATE, 1))
        plan(3, ("split", U_F + 10), ("clip", GATE, 0), ("sum", UP, 0), ("round", GATE, 2), ("clip", GATE, 1),
             ("split", U_F + 11), ("sum", UP, 1), ("clip", GATE, 2), ("round", GATE, 3))
        plan(4, ("split", U_F + 12), ("clip", GATE, 3), ("sum", UP, 2), ("split", U_F + 13), ("sum", UP, 3))
        plan(5, ("split", U_F + 14), ("sum", DOWN, 0), ("mean", UP), ("round", UP, 0), ("round", UP, 1),
             ("clip", UP, 0), ("split", U_F + 15), ("sum", DOWN, 1), ("clip", UP, 1))
        plan(6, ("split", U_F + 16), ("round", UP, 2), ("sum", DOWN, 2), ("clip", UP, 2), ("round", UP, 3),
             ("split", U_F + 17), ("sum", DOWN, 3), ("clip", UP, 3))
        plan(7, ("split", U_F + 18), ("sum", DOWN, 4), ("split", U_F + 19), ("sum", DOWN, 5))
        plan(8, ("mean", DOWN), ("d", 0), ("round", DOWN, 0))
        plan(9, ("d", 1), ("clip", DOWN, 0), ("round", DOWN, 1))
        plan(10, ("d", 2), ("clip", DOWN, 1), ("round", DOWN, 2), ("d", 3), ("clip", DOWN, 2), ("round", DOWN, 3))
        plan(11, ("d", 4), ("clip", DOWN, 3))
        plan(12, ("round", DOWN, 4), ("round", DOWN, 5))
        plan(13, ("clip", DOWN, 4), ("d", 5), ("clip", DOWN, 5), ("d", 6))
        plan(14, ("d", 7))
        plan(15, ("d", 8))
        plan(16, ("d", 9), ("d", 10))
        for u in range(11, D_UNITS):
            plan(17 + u - 11, ("d", u))
        POOL_ROUNDS = (GATE, UP, DOWN)
        POOL_D = [1, 3, 5] + list(range(7, D_UNITS))

        def halves(steps):
            return steps[:2], steps[2:]

        def no_prep(steps):
            pass

        def unit_wait(eng, n):
            if n < U_F:
                eng.wait_ge(got_ws, 16)
            else:
                eng.wait_ge(got_wf[(n - U_F) // 2], 16)

        def d_unit_wait(eng, u):
            if u < NM:
                eng.wait_ge(got_wd[0], 16)
            elif u < D_EARLY:
                eng.wait_ge(got_wd[1], 16)
            else:
                eng.wait_ge(got_wd[2], 32)

        def clipped(eng, m, k):
            eng.wait_ge(bit_clip, 2 * (BIT_BASE[m] + k + 1))

        block = ctx.enter_context(nc.Block())

        @block.sync
        def _(sp):
            x_t = x.rearrange("(n p) h -> n p h", p=P)
            out_t = out.rearrange("(n p) h -> n p h", p=P)

            def load_x(n, s):
                sp.dma_start(xin[:, s, :], x_t[n, :, :]).then_inc(got_x[s], 16)

            def load_res(n, s):
                sp.dma_start(res[:, s, :], x_t[n, :, :]).then_inc(got_res[s], 16)

            def load_f(j):
                sp.dma_start(WF[:, NS + 2 * j + 1:NS + 2 * j + 3, :].rearrange("p u c -> p (u c)").bitcast(F32),
                             w_f[:, 1024 * j:1024 * (j + 1)]).then_inc(got_wf[j], 16)

            def load_bit(m, k):
                raw = BITS[m][k][0]
                if m == DOWN:
                    c0, c1 = DOWN_CHUNKS[k]
                    if c1 - c0 == 1:
                        sp.dma_start(raw, w_bd[P * c0:P * c0 + chunk_rows(c0), :]).then_inc(got_bit[m][k], 16)
                    else:
                        sp.dma_start(raw.rearrange("p (c h) -> p c h", h=H),
                                     w_bd[P * c0:P * c1, :].rearrange("(c p) h -> p c h", p=P)
                                     ).then_inc(got_bit[m][k], 16)
                else:
                    sp.dma_start(raw, (w_bu if m else w_bg)[P * k:P * (k + 1), :]).then_inc(got_bit[m][k], 16)

            load_x(0, 0)
            sp.dma_start(idf[:, :], ident).then_inc(got_ident, 16)
            sp.dma_start(sc[:, :], scal.partition_broadcast(P)).then_inc(got_scalars, 16)
            load_x(1, 1)
            for s in range(2):
                sp.dma_start(h32[:, s, :], x_t[2 + s, :, :]).then_inc(got_first[s], 16)
            sp.dma_start(WF[:, 1:NS + 1, :].rearrange("p u c -> p (u c)").bitcast(F32), w_s).then_inc(got_ws, 16)
            sp.dma_start(lp[:, :], local_point).then_inc(got_lp, 16)
            load_f(0)
            load_bit(GATE, 0)
            load_f(1)
            load_bit(GATE, 1)
            load_f(2)
            load_bit(GATE, 2)
            load_bit(GATE, 3)
            load_f(3)
            load_bit(UP, 0)
            load_bit(UP, 1)
            load_f(4)
            load_bit(UP, 2)
            load_bit(UP, 3)
            load_f(5)
            for k in range(3):
                load_bit(DOWN, k)
            load_f(6)
            sp.wait_ge(xq_tp, TT)
            for k in range(3, PIECES[DOWN]):
                load_bit(DOWN, k)
            for j in range(7, NF - 1):
                load_f(j)
            tail = KC * F_TILES[-1][1]
            sp.dma_start(WF[:, NS + 2 * NF - 1:NS + 2 * NF + 1, :].bitcast(F32)[:, :, 0:tail],
                         w_f_tail.rearrange("p (u c) -> p u c", u=2)).then_inc(got_wf[NF - 1], 16)
            clipped(sp, GATE, PIECES[GATE] - 1)
            sp.dma_start(WD[:, 1:NM + 1, :].rearrange("p u c -> p (u c)").bitcast(F32), w_poly).then_inc(got_wd[0], 16)
            early = (D_EARLY - NM) * P
            sp.dma_start(WD[:, NM + 1:D_EARLY + 1, :].bitcast(F32),
                         w_down[0:early, :].rearrange("(c p) h -> p c h", p=P)).then_inc(got_wd[1], 16)
            clipped(sp, DOWN, PIECES[DOWN] - 1)
            for s in range(2):
                load_x(TT + s, s)
            sp.dma_start(WD[:, D_EARLY + 1:D_UNITS, :].bitcast(F32),
                         w_down[early:(NF - 1) * P, :].rearrange("(c p) h -> p c h", p=P)).then_inc(got_wd[2], 16)
            sp.dma_start(WD[0:D_UNIT_K[-1], D_UNITS, :].bitcast(F32), w_down[(NF - 1) * P:F, :]).then_inc(got_wd[2], 16)
            load_res(0, 0)
            load_res(1, 1)

            def down(b, front):
                for t in range(TT):
                    n = b * TT + t
                    if front and t < 2:
                        sp.wait_ge(xq_tp, TT * (b + 1) + t + 1)
                        load_x(TT * (b + 1) + t + 2, t)
                    sp.wait_ge(pair_free, PER_BLOCK * b + FIRST_D + t + 1)
                    sp.dma_start(out_t[n, :, :], res[:, t % 2, :]).then_inc(stored[t % 2], 16)
                    if front or t < TT - 2:
                        sp.wait_ge(stored[t % 2], 16 * (TT // 2) * b + 16 * (t // 2 + 1))
                        load_res(n + 2, t % 2)

            def next_x(b):
                for t in range(2):
                    sp.wait_ge(xq_tp, TT * b + t + 3)
                    load_x(TT * (b + 1) + t, t)

            with sp.Fori(0, NB - 2) as b:
                down(b, True)
                next_x(b + 1)
            down(NB - 2, True)
            down(NB - 1, False)
            for s in range(2):
                sp.wait_ge(stored[s], TOK // P // 2 * 16)

        @block.gpsimd
        def _(pool):
            pool.wait_ge(const_ready, 1)

            def rstd(n, t):
                pool.wait_ge(stats_v, STATS * n + STATS)
                nc.gpsimd.tensor_tensor(rs[:, t:t + 1], ve[:, t:t + 1], neghalf[:, :], ALU.pow).then_inc(rstd_ready, 1)

            def term_lo(b, m):
                pool.wait_ge(t_hi_ready, NM * b + m + 1)
                nc.gpsimd.tensor_tensor(t_lo[:, m, :], t32[:, m % 2, :], t_hi[:, m, :],
                                        ALU.subtract).then_inc(t_lo_ready, 1)

            def f_lo(b, j):
                rows = F_TILES[j][1]
                pool.wait_ge(h_hi_ready, NF * b + j + 1)
                nc.gpsimd.tensor_tensor(h_lo[0:rows, j, :], h32[0:rows, j % 2, :], h_hi[0:rows, j, :],
                                        ALU.subtract).then_inc(h_lo_ready, 1)

            def d_scale(u):
                d_unit_wait(pool, u)
                raw = raw_unit(WD, u)[0:D_UNIT_K[u], :]
                nc.gpsimd.tensor_scalar(raw, raw, WS, 0.0, ALU.mult, ALU.add).then_inc(wd_scaled, 1)

            def d_lo(u):
                rows = D_UNIT_K[u]
                pool.wait_ge(wd_hi, u + 1)
                nc.gpsimd.tensor_tensor(w_unit(WD, u, 1)[0:rows, :], raw_unit(WD, u)[0:rows, :],
                                        w_unit(WD, u, 0)[0:rows, :], ALU.subtract).then_inc(wd_lo, 1)

            def bit_total(m):
                cols = slice(BIT_BASE[m], BIT_BASE[m] + PIECES[m])
                pool.wait_ge(bit_abs, BIT_BASE[m] + PIECES[m])
                nc.gpsimd.partition_all_reduce(wtot[:, cols], wabs[:, cols], P, RADD).then_inc(bit_tot, 1)

            def bit_rounding(m, k):
                raw, _, rows = BITS[m][k]
                pool.wait_ge(bit_mean, BIT_MEANS * (m + 1))
                nc.gpsimd.tensor_scalar(raw, raw, rw[0:rows, m:m + 1], MAGIC, ALU.mult,
                                        ALU.add).then_inc(bit_round[m], 1)

            def up(b, order, prep):
                for i, (kind, n) in enumerate(order):
                    if kind == "S":
                        for m in range(NM):
                            prep(TERM_PREP.get(m, []))
                            term_lo(b, m)
                    first, rest = halves(PREP.get(i, []))
                    prep(first)
                    if kind == "F":
                        f_lo(b, n)
                    prep(rest)

            def prep(steps):
                for what, *n in steps:
                    if what == "sum" and n[1] == PIECES[n[0]] - 1:
                        bit_total(n[0])
                    elif what == "round" and n[0] in POOL_ROUNDS:
                        bit_rounding(*n)
                    elif what == "d" and n[0] in POOL_D:
                        k = POOL_D.index(n[0])
                        for u in POOL_D[0:2] if k == 0 else POOL_D[k + 1:k + 2]:
                            d_scale(u)
                        d_lo(*n)

            nc.gpsimd.memset(wabs[:, NPIECES - 1:NPIECES], 0.0).then_inc(tail_zero, 1)
            for t in range(TT):
                rstd(t, t)
            up(0, FIRST, prep)
            with pool.Fori(0, NB - 1) as b:
                for t in range(TT):
                    rstd((b + 1) * TT + t, t)
                up(b + 1, STEADY, no_prep)

        @block.scalar
        def _(act):
            def front_abs(b, t):
                n = b * TT + t
                act.wait_ge(xn_ready, n + 1)
                if isinstance(b, int) and b == 0:
                    unused = t_hi[:, t, :]
                else:
                    act.wait_ge(xq_tp, n - 1)
                    unused = xq[:, t % 2, :]
                nc.scalar.activation(unused, x_buffer(b, t), ACT.Abs,
                                     accum_out=xabs[:, t:t + 1]).then_inc(xabs_ready, 1)

            def front_hi(b, t):
                n = b * TT + t
                act.wait_ge(x_tp, n + 1)
                bank = FIRST_X[t] if isinstance(b, int) and b == 0 else tpX
                nc.scalar.copy(xT_hi[:, :, P * t:P * (t + 1)],
                               bank[:, :].rearrange("p (k t) -> p k t", k=KC)).then_inc(xhi_ready, 1)

            def front_q(b, t):
                if isinstance(b, int) and b == 0:
                    bank = FIRST_XQ[t]
                    act.wait_ge(xq_tp, t // 2 * 2 + 2)
                else:
                    bank = tpQ[:, 0:KC * P]
                    act.wait_ge(xq_tp, b * TT + t + 1)
                nc.scalar.copy(xqT[:, :, P * t:P * (t + 1)],
                               bank.rearrange("p (k t) -> p k t", k=KC)).then_inc(xqT_ready, 1)

            def split_hi(n):
                tensor, u, cols, rows = UNITS[n]
                unit_wait(act, n)
                if n:
                    act.wait_ge(w_lo, n)
                nc.scalar.mul(w_unit(tensor, u, 0, 0, cols)[0:rows, :], raw_unit(tensor, u, cols)[0:rows, :],
                              WS).then_inc(w_hi, 1)

            def d_hi(u):
                d_unit_wait(act, u)
                if u:
                    act.wait_ge(wd_lo, u)
                rows = D_UNIT_K[u]
                if u in POOL_D:
                    act.wait_ge(wd_scaled, POOL_D.index(u) + 1)
                    nc.scalar.copy(w_unit(WD, u, 0)[0:rows, :], raw_unit(WD, u)[0:rows, :]).then_inc(wd_hi, 1)
                else:
                    nc.scalar.mul(w_unit(WD, u, 0)[0:rows, :], raw_unit(WD, u)[0:rows, :], WS).then_inc(wd_hi, 1)

            def bit_sum(m, k):
                raw, dst, rows = BITS[m][k]
                n = BIT_BASE[m] + k
                act.wait_ge(got_bit[m][k], 16)
                if n == NPIECES - 1:
                    act.wait_ge(tail_zero, 1)
                nc.scalar.activation(dst, raw, ACT.Abs, accum_out=wabs[0:rows, n:n + 1]).then_inc(bit_abs, 1)

            def bit_rounding(m, k):
                raw, _, rows = BITS[m][k]
                act.wait_ge(bit_mean, BIT_MEANS * (m + 1))
                nc.scalar.activation(raw, raw, ACT.Copy, bias=MAGIC,
                                     scale=rw[0:rows, m:m + 1]).then_inc(bit_round[m], 1)

            def terms(b, prep):
                for m in range(NM):
                    prep(TERM_PREP.get(m, []))
                    act.wait_ge(term_ready, NM * b + m + 1)
                    nc.scalar.copy(t_hi[:, m, :], t32[:, m % 2, :]).then_inc(t_hi_ready, 1)

            def f_gate(b, j, i):
                rows = F_TILES[j][1]
                act.wait_ge(pair_ready, PER_BLOCK * b + i + 1)
                nc.scalar.activation(half[0:rows, i % RING, 0:BLK], bankA[i % RING][0:rows, 0:BLK], ACT.Silu,
                                     scale=1.0 / WS).then_inc(half_ready, 1)

            def f_hi(b, j, i):
                rows = F_TILES[j][1]
                act.wait_ge(pair_free, PER_BLOCK * b + i + 1)
                nc.scalar.copy(h_hi[0:rows, j, :], h32[0:rows, j % 2, :]).then_inc(h_hi_ready, 1)

            def b_gate(b, n, i):
                c = n % NC
                cols = B_COLS[c][1]
                act.wait_ge(pair_ready, PER_BLOCK * b + i + 1)
                nc.scalar.activation(half[:, i % RING, 0:cols], bankA[i % RING][:, 0:cols], ACT.Relu,
                                     scale=wsc[:, 0:1]).then_inc(relu_ready, 1)
                act.wait_ge(relu_ready, TT * NC * b + n + 1)
                nc.scalar.activation(half[:, i % RING, 0:cols], half[:, i % RING, 0:cols],
                                     ACT.Square).then_inc(half_ready, 1)

            def b_round(b, t):
                act.wait_ge(bit_v, BIT * (b * TT + t) + BIT_SCALE)
                nc.scalar.activation(prod, prod, ACT.Copy, bias=MAGIC, scale=qs[:, 0:1]).then_inc(q8_round, 1)

            def up(b, order, prep):
                due = None
                for i, (kind, n) in enumerate(order):
                    first, rest = halves(PREP.get(i, []))
                    if kind == "S":
                        terms(b, prep)
                    elif kind == "F":
                        f_gate(b, n, i)
                    else:
                        b_gate(b, n, i)
                    if due is not None:
                        b_round(b, due)
                        due = None
                    prep(first)
                    if kind == "F":
                        f_hi(b, n, i)
                    prep(rest)
                    if kind == "B" and n % NC == NC - 1:
                        due = n // NC
                b_round(b, due)

            def down(b, front):
                for t in range(TT):
                    n = b * TT + t
                    act.wait_ge(q8_tp, n + 1)
                    nc.scalar.copy(q8T[:, 0:NQ1, :], tpX_b.rearrange("p (c t) -> p c t", t=P))
                    nc.scalar.copy(q8T[:, NQ1:NI - 1, :],
                                   tpQ[:, 0:(NI - 1 - NQ1) * P].rearrange("p (c t) -> p c t", t=P))
                    nc.scalar.copy(q8T[0:I_CHUNKS[-1][1], NI - 1, :],
                                   tpQ[0:I_CHUNKS[-1][1], (NI - 1 - NQ1) * P:(NI - NQ1) * P]).then_inc(q8T_ready, 1)
                    if front:
                        front_abs(b + 1, t)
                        front_hi(b + 1, t)
                        front_q(b + 1, t)

            act.wait_ge(got_ident, 16)
            nc.scalar.copy(idb[:, :], idf[:, :]).then_inc(idb_ready, 1)
            act.wait_ge(expo_ready, 2)
            nc.scalar.activation(ratio[:, :], expo[:, :], ACT.Exp).then_inc(ratio_ready, 1)
            act.wait_ge(const_ready, 1)
            nc.scalar.activation(warm[:, :], neghalf[:, :], ACT.Silu)
            front_abs(0, 0)
            front_hi(0, 0)
            split_hi(0)
            front_hi(0, 1)
            front_abs(0, 1)
            front_hi(0, 2)
            front_abs(0, 2)
            front_hi(0, 3)
            split_hi(1)
            front_abs(0, 3)
            split_hi(U_F)
            split_hi(U_F + 1)

            def prep(steps):
                for what, *n in steps:
                    if what == "split":
                        split_hi(*n)
                    elif what == "d":
                        d_hi(*n)
                    elif what == "sum":
                        bit_sum(*n)
                    elif what == "xq":
                        front_q(0, *n)
                    elif what == "round" and n[0] not in POOL_ROUNDS:
                        bit_rounding(*n)

            up(0, FIRST, prep)
            with act.Fori(0, NB - 1) as b:
                down(b, True)
                up(b + 1, STEADY, no_prep)
            down(NB - 1, False)

        @block.vector
        def _(dve):
            def front_stats(b, t):
                n = b * TT + t
                one = slice(t, t + 1)

                def step(k, ins):
                    ins.then_inc(stats_v, 1)
                    dve.wait_ge(stats_v, STATS * n + k)

                if not (isinstance(b, int) and b == 0):
                    dve.wait_ge(got_x[t % 2], 16 * (TT // 2) * b + 16 * (t // 2))
                elif t < 2:
                    dve.wait_ge(got_x[t], 16)
                else:
                    dve.wait_ge(got_first[t - 2], 16)
                step(1, nc.vector.bn_stats(st6[:, :], x_buffer(b, t)))
                nc.vector.memset(unused[:, :], 0.0)
                step(2, nc.vector.bn_aggr(mv[:, t, :], st6[:, :]))
                nc.vector.tensor_scalar_add(ve[:, one], mv[:, t, 1:2], LN_EPS).then_inc(stats_v, 1)

            def front_xn(b, t):
                xt = x_buffer(b, t)
                dve.wait_ge(rstd_ready, b * TT + t + 1)
                nc.vector.tensor_scalar(xt, xt, mv[:, t, 0:1], rs[:, t:t + 1], ALU.subtract,
                                        ALU.mult).then_inc(xn_ready, 1)

            def front_quant(b, t):
                n = b * TT + t
                one = slice(t, t + 1)
                tmp = t32[:, t % 2, :]

                def step(k, ins):
                    ins.then_inc(quant_v, 1)
                    dve.wait_ge(quant_v, QUANT * n + k)

                dve.wait_ge(xabs_ready, n + 1)
                nc.vector.tensor_scalar_mul(beta[:, one], xabs[:, one], 1.0 / H)
                step(1, nc.vector.tensor_scalar(beta_e[:, one], xabs[:, one], 1.0 / H, Q_EPS, ALU.mult, ALU.add))
                step(2, nc.vector.reciprocal(rbeta[:, one], beta_e[:, one]))
                step(3, nc.vector.tensor_scalar(tmp, x_buffer(b, t), rbeta[:, one], SQRT7, ALU.mult, ALU.mult))
                step(4, nc.vector.tensor_scalar(tmp, tmp, MAGIC, MAGIC - 8.0, ALU.add, ALU.max))
                nc.vector.tensor_scalar(xq_buffer(b, t), tmp, MAGIC + 7.0, MAGIC, ALU.min,
                                        ALU.subtract).then_inc(quant_v, 1)

            def front_lo(b, t):
                dve.wait_ge(xhi_ready, b * TT + t + 1)
                part = xT_hi[:, :, P * t:P * (t + 1)]
                bank = FIRST_X[t] if isinstance(b, int) and b == 0 else tpX
                nc.vector.tensor_tensor(xT_lo[:, :, P * t:P * (t + 1)],
                                        bank[:, :].rearrange("p (k t) -> p k t", k=KC), part,
                                        ALU.subtract).then_inc(xlo_ready, 1)

            def split_lo(n):
                tensor, u, cols, rows = UNITS[n]
                dve.wait_ge(w_hi, n + 1)
                nc.vector.scalar_tensor_tensor(w_unit(tensor, u, 1, 0, cols)[0:rows, :],
                                               raw_unit(tensor, u, cols)[0:rows, :], WS,
                                               w_unit(tensor, u, 0, 0, cols)[0:rows, :],
                                               ALU.mult, ALU.subtract).then_inc(w_lo, 1)

            def d_lo(u):
                rows = D_UNIT_K[u]
                dve.wait_ge(wd_hi, u + 1)
                nc.vector.scalar_tensor_tensor(w_unit(WD, u, 1)[0:rows, :], raw_unit(WD, u)[0:rows, :], WS,
                                               w_unit(WD, u, 0)[0:rows, :], ALU.mult,
                                               ALU.subtract).then_inc(wd_lo, 1)

            def bit_means(m):
                one = slice(m, m + 1)
                count = I * H

                def step(k, ins):
                    ins.then_inc(bit_mean, 1)
                    dve.wait_ge(bit_mean, BIT_MEANS * m + k)

                dve.wait_ge(bit_tot, m + 1)
                step(1, nc.vector.tensor_reduce(wsum[:, one], wtot[:, BIT_BASE[m]:BIT_BASE[m] + PIECES[m]],
                                                AX_X, ALU.add))
                nc.vector.tensor_scalar_mul(wmean[:, one], wsum[:, one], 1.0 / count).then_inc(bit_mean, 1)
                step(3, nc.vector.tensor_scalar(wmean_e[:, one], wsum[:, one], 1.0 / count, Q_EPS, ALU.mult,
                                                ALU.add))
                nc.vector.tensor_tensor(wsc[:, one], wmean[:, one], sc[:, BIT_SCAL[m]:BIT_SCAL[m] + 1], ALU.mult)
                nc.vector.reciprocal(rw[:, one], wmean_e[:, one]).then_inc(bit_mean, 1)

            def bit_clipping(m, k):
                raw, dst, _ = BITS[m][k]
                dve.wait_ge(bit_round[m], k + 1)
                nc.vector.tensor_scalar(dst, raw, MAGIC, 1.0, ALU.subtract, ALU.min).then_inc(bit_clip, 1)
                dve.wait_ge(bit_clip, 2 * (BIT_BASE[m] + k) + 1)
                nc.vector.tensor_scalar_max(dst, dst, -1.0).then_inc(bit_clip, 1)

            def terms(b, i, prep):
                a, g = bankA[i % RING], bankB[i % RING]
                free = PER_BLOCK * b + i + 1

                dve.wait_ge(pair_ready, free)
                nc.vector.tensor_scalar_mul(t32[:, 0, :], a[:, :], 1.0 / WS).then_inc(term_ready, 1)
                nc.vector.tensor_scalar(delta[:, :], g[:, :], 1.0 / WS, lp[:, 0:1], ALU.mult,
                                        ALU.subtract).then_inc(pair_free, 1)
                dve.wait_ge(pair_free, free)
                for m in range(1, NM):
                    prep(TERM_PREP.get(m, []))
                    if m == 5:
                        dve.wait_ge(term_ready, NM * b + m)
                        nc.vector.scalar_tensor_tensor(delta[:, :], delta[:, :], THD, delta[:, :], ALU.is_le,
                                                       ALU.mult).then_inc(keep_v, 1)
                        dve.wait_ge(keep_v, 2 * b + 1)
                        nc.vector.scalar_tensor_tensor(delta[:, :], delta[:, :], -THD, delta[:, :], ALU.is_ge,
                                                       ALU.mult).then_inc(keep_v, 1)
                        dve.wait_ge(keep_v, 2 * b + 2)
                    dve.wait_ge(term_ready, NM * b + m)
                    if m >= 2:
                        dve.wait_ge(t_lo_ready, NM * b + m - 1)
                    nc.vector.scalar_tensor_tensor(t32[:, m % 2, :], delta[:, :], ratio[:, m - 1:m],
                                                   t32[:, (m - 1) % 2, :], ALU.mult,
                                                   ALU.mult).then_inc(term_ready, 1)

            def f_product(b, j, i):
                rows = F_TILES[j][1]
                dve.wait_ge(half_ready, half_count(b, i))
                if j >= 2:
                    dve.wait_ge(h_lo_ready, NF * b + j - 1)
                nc.vector.scalar_tensor_tensor(h32[0:rows, j % 2, :], bankB[i % RING][0:rows, :], 1.0 / WS,
                                               half[0:rows, i % RING, :], ALU.mult, ALU.mult).then_inc(pair_free, 1)

            def half_count(b, i):
                return (NF + TT * NC) * b + i

            def b_product(b, n, i):
                o, cols = B_COLS[n % NC]
                dve.wait_ge(half_ready, half_count(b, i))
                nc.vector.tensor_tensor(prod[:, o:o + cols], bankB[i % RING][:, 0:cols],
                                        half[:, i % RING, 0:cols], ALU.mult).then_inc(pair_free, 1)
                if n % NC == NC - 1:
                    dve.wait_ge(pair_free, PER_BLOCK * b + i + 1)
                    b_scale(b, n // NC)

            def b_scale(b, t):
                def step(k, ins):
                    ins.then_inc(bit_v, 1)
                    dve.wait_ge(bit_v, BIT * (b * TT + t) + k)

                bt = beta[:, t:t + 1]
                nc.vector.tensor_tensor(b2[:, :], bt, bt, ALU.mult).then_inc(bit_v, 1)
                step(2, nc.vector.tensor_reduce(pmax[:, :], prod, AX_X, ALU.max, apply_absolute_value=True))
                step(3, nc.vector.scalar_tensor_tensor(cB[:, :], bt, wsc[:, 1:2], b2[:, :], ALU.mult, ALU.mult))
                step(4, nc.vector.scalar_tensor_tensor(cBa[:, :], cB[:, :], -1.0, cB[:, :], ALU.mult, ALU.max))
                nc.vector.tensor_tensor(gam[:, :], cBa[:, :], pmax[:, :], ALU.mult)
                step(5, nc.vector.tensor_scalar(game[:, :], cBa[:, :], pmax[:, :], Q_EPS, ALU.mult, ALU.add))
                nc.vector.tensor_scalar(od[:, t:t + 1], gam[:, :], 1.0 / 127.0, wsc[:, 2:3], ALU.mult, ALU.mult)
                step(6, nc.vector.reciprocal(rgam[:, :], game[:, :]))
                step(7, nc.vector.tensor_scalar(qs[:, :], rgam[:, :], 127.0, cB[:, :], ALU.mult, ALU.mult))

            def b_store(b, t):
                base = BIT * (b * TT + t)
                dve.wait_ge(q8_round, b * TT + t + 1)
                nc.vector.tensor_scalar(q8[:, t, :], prod, MAGIC, 127.0, ALU.subtract, ALU.min).then_inc(bit_v, 1)
                dve.wait_ge(bit_v, base + 8)
                nc.vector.tensor_scalar_max(q8[:, t, :], q8[:, t, :], -128.0).then_inc(bit_v, 1)

            def up(b, order, prep):
                for i, (kind, n) in enumerate(order):
                    steps = PREP.get(i, [])
                    if kind == "S":
                        terms(b, i, prep)
                    elif kind == "F":
                        f_product(b, n, i)
                    else:
                        if n % NC == 0 and n > 0:
                            prep(steps)
                            steps = []
                            b_store(b, n // NC - 1)
                            dve.wait_ge(bit_v, BIT * (b * TT + n // NC) - 1)
                        b_product(b, n, i)
                    prep(steps)
                b_store(b, TT - 1)

            def down(b, is_front):
                for t in range(TT):
                    n = b * TT + t
                    i = FIRST_D + t
                    if is_front:
                        front_stats(b + 1, t)
                        front_xn(b + 1, t)
                        front_quant(b + 1, t)
                        front_lo(b + 1, t)
                    dve.wait_ge(got_res[t % 2], 16 * (TT // 2) * b + 16 * (t // 2 + 1))
                    dve.wait_ge(pair_ready, PER_BLOCK * b + i + 1)
                    nc.vector.scalar_tensor_tensor(res[:, t % 2, :], bankA[i % RING][:, :], 1.0 / WS,
                                                   res[:, t % 2, :], ALU.mult, ALU.add).then_inc(out_v, 1)
                    dve.wait_ge(out_v, n + 1)
                    nc.vector.scalar_tensor_tensor(res[:, t % 2, :], bankB[i % RING][:, :], od[:, t:t + 1],
                                                   res[:, t % 2, :], ALU.mult, ALU.add).then_inc(pair_free, 1)

            nc.vector.memset(neghalf[:, :], -0.5).then_inc(const_ready, 1)
            front_stats(0, 0)
            dve.wait_ge(got_scalars, 16)
            nc.vector.tensor_scalar_mul(expo[:, 0:1], sc[:, 3:4], -1.0).then_inc(expo_ready, 1)
            nc.vector.tensor_tensor(expo[:, 1:G], sc[:, 3:2 + G], sc[:, 4:3 + G], ALU.subtract).then_inc(expo_ready, 1)
            for t in range(1, TT):
                front_stats(0, t)
                front_xn(0, t - 1)
            front_lo(0, 0)
            front_xn(0, TT - 1)
            front_lo(0, 1)
            split_lo(0)
            front_lo(0, 2)
            front_lo(0, 3)
            split_lo(1)
            front_quant(0, 0)
            split_lo(U_F)
            front_quant(0, 1)
            split_lo(U_F + 1)
            front_quant(0, 2)
            front_quant(0, 3)
            dve.wait_ge(ratio_ready, 1)
            dve.wait_ge(got_lp, 16)

            def prep(steps):
                for what, *n in steps:
                    if what == "split":
                        split_lo(*n)
                    elif what == "d" and n[0] not in POOL_D:
                        d_lo(*n)
                    elif what == "mean":
                        bit_means(*n)
                    elif what == "clip":
                        bit_clipping(*n)

            up(0, FIRST, prep)
            with dve.Fori(0, NB - 1) as b:
                down(b, True)
                up(b + 1, STEADY, no_prep)
            down(NB - 1, False)

        @block.tensor
        def _(pe):
            def split_product(bank, w, xx, ks, last_of_all=True, first=True):
                for k in ks:
                    for wp, xp in ((0, 0), (0, 1), (1, 0)):
                        ins = nc.tensor.matmul(bank, w(wp, k), xx(xp, k),
                                               start=(first and k == ks[0] and (wp, xp) == (0, 0)),
                                               stop=(last_of_all and k == ks[-1] and wp == 1))
                return ins

            def xT(part, k):
                return (xT_lo if part else xT_hi)[:, k, :]

            def free(b, i):
                if not (isinstance(b, int) and PER_BLOCK * b + i < RING):
                    pe.wait_ge(pair_free, PER_BLOCK * b + i - RING + 1)

            def x_transposes(b, t):
                n = b * TT + t
                pe.wait_ge(xn_ready, n + 1)
                bank = tpX
                if isinstance(b, int) and b == 0:
                    bank = FIRST_X[t]
                for k in range(KC):
                    ins = nc.tensor.transpose(bank[:, P * k:P * (k + 1)], x_buffer(b, t)[:, P * k:P * (k + 1)],
                                              idf[:, :])
                ins.then_inc(x_tp, 1)

            def xq_transposes(b, t):
                pe.wait_ge(quant_v, QUANT * (b * TT + t) + QUANT)
                bank = FIRST_XQ[t] if isinstance(b, int) and b == 0 else tpQ[:, 0:KC * P]
                for k in range(KC):
                    ins = nc.tensor.transpose(bank[:, P * k:P * (k + 1)], xq_buffer(b, t)[:, P * k:P * (k + 1)], idb[:, :])
                ins.then_inc(xq_tp, 1)

            def s_pair(b, i):
                free(b, i)
                pe.wait_ge(xlo_ready, TT * (b + 1))
                pe.wait_ge(w_lo, 1)
                split_product(bankA[i % RING][:, :], lambda q, k: w_unit(WF, 0, q, P * k, P), xT, range(KC))
                pe.wait_ge(w_lo, 2)
                split_product(bankB[i % RING][:, :], lambda q, k: w_unit(WF, 1, q, P * k, P), xT,
                              range(KC)).then_inc(pair_ready, 1)

            def f_pair(b, j, i, first_use):
                n = F_TILES[j][1]
                free(b, i)
                if first_use:
                    pe.wait_ge(w_lo, U_F + 2 * j + 2)
                split_product(bankA[i % RING][0:n, :], lambda q, k: w_unit(WF, NS + 2 * j, q, n * k, n), xT, range(KC))
                split_product(bankB[i % RING][0:n, :], lambda q, k: w_unit(WF, NS + 2 * j + 1, q, n * k, n), xT,
                              range(KC)).then_inc(pair_ready, 1)

            def b_pair(b, m, i, first_use):
                t = m // NC
                o, n = B_COLS[m % NC]
                free(b, i)
                if m == 0:
                    pe.wait_ge(xqT_ready, TT * (b + 1))
                    if first_use:
                        clipped(pe, UP, PIECES[UP] - 1)
                for side, bank in ((0, bankA[i % RING]), (1, bankB[i % RING])):
                    for k in range(KC):
                        ins = nc.tensor.matmul(bank[:, 0:n], xqT[:, k, P * t:P * (t + 1)],
                                               WB[:, side, I * k + o:I * k + o + n],
                                               start=(k == 0), stop=(k == KC - 1))
                ins.then_inc(pair_ready, 1)

            def up(b, order, first_use):
                for i, (kind, n) in enumerate(order):
                    if kind == "S":
                        s_pair(b, i)
                    elif kind == "F":
                        f_pair(b, n, i, first_use)
                    else:
                        b_pair(b, n, i, first_use)
                    if first_use and 1 <= i <= 2:
                        for t in (2 * i - 2, 2 * i - 1):
                            xq_transposes(b, t)

            def down(b, front, first_use=False):
                for t in range(TT):
                    n = b * TT + t
                    i = FIRST_D + t
                    free(b, i)
                    tok = slice(P * t, P * (t + 1))

                    def act_part(q, u):
                        if u < NM:
                            return (t_lo if q else t_hi)[:, u, tok]
                        kk = F_TILES[u - NM][1]
                        return (h_lo if q else h_hi)[0:kk, u - NM, tok]

                    def w_part(q, u):
                        return w_unit(WD, u, q)[0:D_UNIT_K[u], :]

                    if t == 0:
                        pe.wait_ge(t_lo_ready, NM * (b + 1))
                    bank = bankA[i % RING][:, :]
                    for u in range(NM):
                        if first_use and t == 0:
                            pe.wait_ge(wd_lo, u + 1)
                        split_product(bank, act_part, w_part, [u], last_of_all=False, first=(u == 0))
                    pe.wait_ge(bit_v, BIT * n + BIT)
                    if front or t == 0:
                        pe.wait_ge(xlo_ready, n + TT)
                        pe.wait_ge(xqT_ready, n + TT)
                    for c, (o, kk) in enumerate(I_CHUNKS):
                        to = tpX_b[0:kk, P * c:P * (c + 1)] if c < NQ1 else tpQ[0:kk, P * (c - NQ1):P * (c - NQ1 + 1)]
                        ins = nc.tensor.transpose(to, q8[:, t, o:o + kk], idb[:, :])
                    ins.then_inc(q8_tp, 1)
                    if t == 0:
                        pe.wait_ge(h_lo_ready, NF * (b + 1))
                    for u in range(NM, D_UNITS):
                        if first_use and t == 0:
                            pe.wait_ge(wd_lo, u + 1)
                        split_product(bank, act_part, w_part, [u], last_of_all=(u == D_UNITS - 1), first=False)
                    pe.wait_ge(q8T_ready, n + 1)
                    if front:
                        x_transposes(b + 1, t)
                        xq_transposes(b + 1, t)
                    if first_use and t == 0:
                        clipped(pe, DOWN, PIECES[DOWN] - 1)
                    for c, (o, kk) in enumerate(I_CHUNKS):
                        ins = nc.tensor.matmul(bankB[i % RING][:, :], q8T[0:kk, c, :], WBD[0:kk, c, :],
                                               start=(c == 0), stop=(c == NI - 1))
                    ins.then_inc(pair_ready, 1)

            pe.wait_ge(got_ident, 16)
            for t in range(TT):
                x_transposes(0, t)
            pe.wait_ge(idb_ready, 1)
            up(0, FIRST, True)
            down(0, True, True)
            up(1, STEADY, False)
            with pe.Fori(1, NB - 1) as b:
                down(b, True)
                up(b + 1, STEADY, False)
            down(NB - 1, False)


def kernel(**inputs):
    import numpy as np
    import concourse.bacc as bacc
    from concourse.bass_utils import run_bass_kernel_spmd

    def get(name):
        return np.asarray(inputs["L0_" + name])

    x = get("attn_hidden_states")
    B, T, H = x.shape
    KC = H // P

    def chunked(w):
        return w.T.reshape(KC, P, w.shape[0]).transpose(1, 0, 2)

    def flat(*parts):
        return np.ascontiguousarray(np.concatenate([a.reshape(a.shape[0], -1) for a in parts], axis=1))

    gate, up = chunked(get("attn_ffn_gate_w")), chunked(get("attn_ffn_up_w"))
    F = gate.shape[2]
    whole = F // P * P
    fuse = get("attn_fuse_weight")
    arrays = {
        "x": np.ascontiguousarray(x.reshape(B * T, H)),
        "w_s": flat(chunked(get("attn_up_w")), chunked(get("attn_gate_w"))),
        "w_f": flat(*[w[:, :, o:o + P] for o in range(0, whole, P) for w in (gate, up)]),
        "w_f_tail": flat(gate[:, :, whole:], up[:, :, whole:]),
        "w_poly": flat(get("attn_local_approx_output").T, fuse.transpose(1, 2, 0)),
        "w_down": np.ascontiguousarray(get("attn_ffn_down_w").T),
        "w_bg": np.ascontiguousarray(get("ffn_w_gate").T),
        "w_bu": np.ascontiguousarray(get("ffn_w_up").T),
        "w_bd": np.ascontiguousarray(get("ffn_w_down").T),
        "local_point": np.ascontiguousarray(get("attn_local_point").reshape(-1, 1)),
        "scal": np.concatenate([get("ffn_s_gate"), get("ffn_s_up"), get("ffn_s_down"),
                                get("attn_discount_factor")]),
        "ident": np.eye(P, dtype=np.float32),
    }
    nc = bacc.Bacc("TRN2", target_bir_lowering=False, num_devices=1)
    arrays = {"in_" + n: a for n, a in arrays.items()}
    args = [nc.dram_tensor(n, a.shape, mybir.dt.from_np(a.dtype), kind="ExternalInput").ap()
            for n, a in arrays.items()]
    args.append(nc.dram_tensor("y", (B * T, H), F32, kind="ExternalOutput").ap())
    bass_kernel(nc, *args)
    r = run_bass_kernel_spmd(nc, [arrays], core_ids=[0])
    return r.results[0]["y"].reshape(B, T, H)
```

```python
import concourse.bass as bass
from concourse import mybir
from concourse.alu_op_type import AluOpType as ALU
from contextlib import ExitStack

ACT = mybir.ActivationFunctionType
F32 = mybir.dt.float32
F16 = mybir.dt.float16
BF16 = mybir.dt.bfloat16
AX_X = mybir.AxisListType.X
RADD = bass.bass_isa.ReduceOp.add

P = 128
MAGIC = 12582912.0
LN_EPS = 1e-5
Q_EPS = 1e-5
SQRT7 = 7.0 ** 0.5
THD = 2.5
WS = 64.0
RING = 3


def spans(n, step):
    return [(o, min(step, n - o)) for o in range(0, n, step)]


def bass_kernel(nc, x, w_s, w_f, w_f_tail, w_poly, w_down, w_bg, w_bu, w_bd, local_point, scal, ident, out):
    TOK, H = x.shape
    S = local_point.shape[0]
    G = w_poly.shape[1] // H - 1
    F = w_down.shape[0]
    I = w_bg.shape[1]
    BLK = 512
    NB = TOK // BLK
    TT = BLK // P
    KC = H // P
    F_TILES = spans(F, P)
    NF = len(F_TILES)
    I_CHUNKS = spans(I, P)
    NI = len(I_CHUNKS)
    B_COLS = spans(I, 512)
    NC = len(B_COLS)
    NM = G + 1
    D_UNITS = NM + NF
    assert S == P and BLK <= 512 and H == 512 and G == 6

    PER_BLOCK = 1 + NF + TT * NC + TT
    assert PER_BLOCK % RING == 0
    FIRST_D = PER_BLOCK - TT
    STEADY = [("S", 0)]
    for n in range(max(NF, TT * NC)):
        STEADY += [("F", n)] * (n < NF) + [("B", n)] * (n < TT * NC)
    FIRST = []
    for kind in "SFFFFFFBBBBBFBFBFBBFBBB":
        FIRST.append((kind, sum(k == kind for k, _ in FIRST)))

    STATS = 3
    QUANT = 5
    BIT = 9
    BIT_SCALED = 7

    ctx = ExitStack()
    with ctx:
        def sb(name, shape, dt):
            return ctx.enter_context(nc.sbuf_tensor(name, shape, dt))

        def sem(name):
            return ctx.enter_context(nc.semaphore(name))

        PIECES = [KC, KC, 6]
        NPIECES = sum(PIECES)
        NS = 2
        WF = sb("w_sf_split", [P, NS + 2 * NF + 1, 1024], F16)
        WD = sb("w_d_split", [P, D_UNITS + 1, 1024], F16)
        WB = sb("w_bit", [P, 2, KC * I], BF16)
        WBD = sb("w_bit_down", [P, NI, H], BF16)
        REGION = sb("region", [P, KC * I + H], F32)
        o = 0
        prod = REGION[:, o:o + I]
        o += I
        q8 = REGION[:, o:o + TT * I // 2].bitcast(BF16).rearrange("p (t i) -> p t i", t=TT)
        o += TT * I // 2
        q8T = REGION[:, o:o + NI * P // 2].bitcast(BF16).rearrange("p (c t) -> p c t", c=NI)
        o += NI * P // 2
        res = REGION[:, o:o + 2 * H].rearrange("p (s h) -> p s h", s=2)
        assert KC * I + H >= o + 2 * H

        xT_hi = sb("xT_hi", [P, KC, BLK], F16)
        xT_lo = sb("xT_lo", [P, KC, BLK], F16)
        xqT = sb("xqT", [P, KC, BLK], BF16)
        xin = sb("xin", [P, 2, H], F32)
        xq = sb("xq", [P, 2, H], BF16)
        xq_words = xq[:, :, :].rearrange("p s h -> p (s h)").bitcast(F32)
        h_hi = sb("h_hi", [P, NF, BLK], F16)
        h_lo = sb("h_lo", [P, NF, BLK], F16)
        t_hi = sb("t_hi", [P, NM, BLK], F16)
        t_lo = sb("t_lo", [P, NM, BLK], F16)
        half = sb("act_half", [P, RING, 512], F32)
        h32 = sb("h32", [P, 2, BLK], F32)
        t32 = sb("t32", [P, 2, BLK], F32)
        delta = sb("delta", [P, BLK], F32)
        idf = sb("ident_f32", [P, P], F32)
        idh = idf[:, 0:P // 2].bitcast(F16)
        idb = sb("ident_bf16", [P, P], BF16)
        sc = sb("scalars", [P, 3 + G], F32)
        lp = sb("local_point", [P, 1], F32)
        st6 = sb("st6", [P, 6], F32)
        unused = sb("unused", [P, 1], F32)
        mv = sb("mean_var", [P, TT, 2], F32)
        ve = sb("var_eps", [P, TT], F32)
        rs = sb("rstd", [P, TT], F32)
        warm = sb("warm", [P, 1], F32)
        neghalf = sb("neg_half", [P, 1], F32)
        xabs = sb("x_abs_sum", [P, TT], F32)
        beta = sb("beta", [P, TT], F32)
        beta_e = sb("beta_eps", [P, TT], F32)
        rbeta = sb("r_beta", [P, TT], F32)
        b2 = sb("beta_sq", [P, 1], F32)
        cB = sb("prod_scale", [P, 1], F32)
        cBa = sb("prod_scale_abs", [P, 1], F32)
        pmax = sb("prod_max", [P, 1], F32)
        gam = sb("gamma", [P, 1], F32)
        game = sb("gamma_eps", [P, 1], F32)
        rgam = sb("r_gamma", [P, 1], F32)
        qs = sb("q_scale", [P, 1], F32)
        od = sb("out_scale", [P, TT], F32)
        expo = sb("expo", [P, G], F32)
        ratio = sb("ratio", [P, G], F32)
        wabs = sb("w_abs_sum", [P, NPIECES], F32)
        wtot = sb("w_abs_total", [P, NPIECES], F32)
        wsum = sb("w_abs_whole", [P, 3], F32)
        wmean = sb("w_mean", [P, 3], F32)
        wmean_e = sb("w_mean_eps", [P, 3], F32)
        rw = sb("r_w_mean", [P, 3], F32)
        wsc = sb("w_scale", [P, 3], F32)

        bankA = [ctx.enter_context(nc.psum_tensor(f"pair_a{n}", [P, 512], F32)) for n in range(RING)]
        bankB = [ctx.enter_context(nc.psum_tensor(f"pair_b{n}", [P, 512], F32)) for n in range(RING)]
        tpX = ctx.enter_context(nc.psum_tensor("tp_x", [P, 512], F32))
        tpQ = ctx.enter_context(nc.psum_tensor("tp_q", [P, 1024], BF16))
        NQ1 = 8
        tpX_b = tpX[:, :].bitcast(BF16)
        tpX_h = tpX[:, :].bitcast(F16)
        FIRST_X = [tpX, bankA[1], bankB[1], bankA[2]]
        FIRST_XQ = [tpQ[:, 0:H], tpQ[:, H:2 * H], tpX_b[:, 0:H], tpX_b[:, H:2 * H]]

        got_x = [sem(f"got_x{s}") for s in range(2)]
        got_first = [sem(f"got_first{s}") for s in range(2)]
        got_res = [sem(f"got_res{s}") for s in range(2)]
        stored = [sem(f"stored{s}") for s in range(2)]
        got_scalars = sem("got_scalars")
        got_lp = sem("got_local_point")
        got_ident = sem("got_ident")
        got_ws = sem("got_ws")
        got_wf = [sem(f"got_wf{j}") for j in range(NF)]
        got_bit = [[sem(f"got_bit{m}_{k}") for k in range(PIECES[m])] for m in range(3)]
        got_wd = [sem(f"got_wd{n}") for n in range(3)]
        const_ready = sem("const_ready")
        idb_ready = sem("idb_ready")
        idh_ready = sem("idh_ready")
        xs_hi = sem("x_split_hi")
        xs_lo = sem("x_split_lo")
        expo_ready = sem("expo_ready")
        ratio_ready = sem("ratio_ready")
        stats_v = sem("stats_v")
        xn_ready = sem("xn_ready")
        quant_v = sem("quant_v")
        rstd_ready = sem("rstd_ready")
        xabs_ready = sem("xabs_ready")
        x_tp = sem("x_transposed")
        xq_tp = sem("xq_transposed")
        xhi_ready = sem("xhi_ready")
        xlo_ready = sem("xlo_ready")
        xqT_ready = sem("xqT_ready")
        w_hi = sem("w_hi")
        w_scaled = sem("w_scaled")
        w_lo = sem("w_lo")
        wd_hi = sem("wd_hi")
        wd_scaled = sem("wd_scaled")
        wd_lo = sem("wd_lo")
        zeros_ready = sem("zeros_ready")
        tail_zero = sem("tail_zero")
        bit_abs = sem("bit_abs")
        bit_tot = sem("bit_tot")
        bit_mean = sem("bit_mean")
        bit_round = [sem(f"bit_round{m}") for m in range(3)]
        bit_clip = sem("bit_clip")
        pair_ready = sem("pair_ready")
        pair_free = sem("pair_free")
        relu_ready = sem("relu_ready")
        half_ready = sem("half_ready")
        term_ready = sem("term_ready")
        keep_v = sem("keep_v")
        t_hi_ready = sem("t_hi_ready")
        t_lo_ready = sem("t_lo_ready")
        h_hi_ready = sem("h_hi_ready")
        h_lo_ready = sem("h_lo_ready")
        bit_v = sem("bit_v")
        q8_round = sem("q8_round")
        q8_tp = sem("q8_transposed")
        q8T_ready = sem("q8T_ready")
        float_ready = sem("float_ready")
        out_v = sem("out_v")

        def x_buffer(b, t):
            if isinstance(b, int) and b == 0 and t < 2:
                return h32[:, t, :]
            return xin[:, t % 2, :]

        def x_part(t, part):
            return half[:, t % 2, :].bitcast(F16)[:, H * part:H * (part + 1)]

        def xq_buffer(b, t):
            if isinstance(b, int) and b == 0 and t < 2:
                return h_lo[:, 2 + t, :].bitcast(BF16)
            return xq[:, t % 2, :]

        def w_unit(t, u, part, lo=0, n=512):
            return t[:, u, 512 * part + lo:512 * part + lo + n]

        def raw_unit(t, u, n=512):
            return t[:, u + 1, :].bitcast(F32)[:, 0:n]

        S_UNITS = [(WF, u, 512, P) for u in range(NS)]
        F_UNITS = [(WF, NS + u, KC * F_TILES[u // 2][1], P) for u in range(2 * NF)]
        UNITS = S_UNITS + F_UNITS
        U_F = NS
        D_UNIT_K = [P] * NM + [n for _, n in F_TILES]
        D_EARLY = 10

        def chunk_rows(c):
            return I_CHUNKS[c][1]

        WD_words = WD[:, :, :].rearrange("p u c -> p (u c)").bitcast(F32)
        WBD_cols = WBD[:, :, :].rearrange("p c h -> p (c h)")
        BITS = [
            [(WD_words[:, I * k:I * (k + 1)], WB[:, 0, I * k:I * (k + 1)], P) for k in range(KC)],
            [(REGION[:, I * k:I * (k + 1)], WB[:, 1, I * k:I * (k + 1)], P) for k in range(KC)],
            [],
        ]
        FREE = (D_EARLY + 1) * H
        assert KC * I <= FREE
        DOWN_CHUNKS = [(0, 3), (3, 5), (5, 7), (7, 9), (9, 10), (10, 11)]
        assert len(DOWN_CHUNKS) == PIECES[2] and DOWN_CHUNKS[-1][1] == NI and D_UNITS + 1 - D_EARLY - 1 == 7
        for c0, c1 in DOWN_CHUNKS:
            if c1 <= 7:
                raw = WD_words[:, FREE + H * c0:FREE + H * c1]
            elif c1 <= 9:
                raw = xin[:, :, :].rearrange("p s h -> p (s h)")
            elif c1 <= 10:
                raw = xq_words
            else:
                raw = REGION[0:chunk_rows(c0), KC * I:KC * I + H]
            BITS[2].append((raw, WBD_cols[0:chunk_rows(c0), H * c0:H * c1], chunk_rows(c0)))
        BIT_BASE = [0, PIECES[0], PIECES[0] + PIECES[1]]
        BIT_MEANS = 4

        GATE, UP, DOWN = 0, 1, 2
        PREP_FIRST = [("split", 2), ("split", 3), ("quant", 0), ("sum", GATE, 0), ("split", 4)]
        PREP = {
            0: [("sum", GATE, 1), ("term", 1), ("split", 5), ("sum", GATE, 2), ("quant", 1), ("term", 2),
                ("term", 3), ("quant", 2)],
            1: [("sum", GATE, 3), ("hi",), ("term", 4), ("mean", GATE), ("split", 6), ("split", 7),
                ("round", GATE, 0), ("round", GATE, 1), ("sum", UP, 0), ("term", 5), ("quant", 3),
                ("split", 8), ("round", GATE, 2), ("round", GATE, 3)],
            2: [("sum", UP, 1), ("split", 9), ("sum", UP, 2), ("clip", GATE, 0), ("split", 10), ("sum", UP, 3),
                ("xq", 0), ("split", 11), ("xq", 1), ("term", 6), ("clip", GATE, 1), ("clip", GATE, 2),
                ("hi",), ("mean", UP), ("round", UP, 0)],
            3: [("round", UP, 1), ("split", 12)],
            4: [("xq", 2), ("clip", GATE, 3), ("split", 13), ("sum", DOWN, 0), ("xq", 3), ("round", UP, 2),
                ("clip", UP, 0), ("clip", UP, 1), ("clip", UP, 2), ("sum", DOWN, 1), ("sum", DOWN, 2),
                ("round", UP, 3), ("clip", UP, 3), ("split", 14), ("sum", DOWN, 3), ("sum", DOWN, 4)],
            5: [("sum", DOWN, 5), ("round", DOWN, 0), ("mean", DOWN), ("split", 15)],
            6: [("split", 16), ("clip", DOWN, 0)],
            8: [("d", 0), ("round", DOWN, 1), ("round", DOWN, 2)],
            9: [("split", 17), ("d", 1), ("split", 18), ("round", DOWN, 3), ("clip", DOWN, 1)],
            11: [("clip", DOWN, 2), ("d", 2)],
            12: [("round", DOWN, 4), ("split", 19), ("round", DOWN, 5), ("d", 3), ("hi",), ("clip", DOWN, 3),
                 ("split", 20), ("clip", DOWN, 4), ("clip", DOWN, 5), ("d", 4)],
            13: [("split", 21), ("d", 5), ("d", 6)],
            14: [("d", 7)],
            16: [("d", 8)],
            17: [("d", 9)],
            18: [("d", 10), ("d", 11)],
            19: [("d", 12)],
            20: [("d", 13)],
            22: [("d", 14), ("d", 15), ("d", 16)],
        }
        POOL_SPLIT = (3, 4, 5, 7, 11, 14, 17, 18, 20)
        POOL_D = (2, 3, 5, 7, 9, 10, 11, 12, 13, 14, 15, 16)
        LOADS = [("bit", GATE, 0), ("f", 0), ("f", 1), ("bit", GATE, 1), ("bit", GATE, 2), ("f", 2), ("bit", GATE, 3),
                 ("f", 3), ("bit", UP, 0), ("f", 4), ("bit", UP, 1), ("bit", UP, 2), ("f", 5), ("bit", UP, 3),
                 ("f", 6), ("bit", DOWN, 0), ("bit", DOWN, 1), ("bit", DOWN, 2), ("bit", DOWN, 3),
                 ("bit", DOWN, 4), ("f", 7), ("bit", DOWN, 5), ("f", 8), ("f", 9)]

        def halves(steps):
            k = steps.index(("hi",)) if ("hi",) in steps else len(steps)
            return steps[:k], steps[k:]

        def no_prep(steps):
            pass

        def unit_wait(eng, n):
            if n < U_F:
                eng.wait_ge(got_ws, 16)
            else:
                eng.wait_ge(got_wf[(n - U_F) // 2], 16)

        def d_unit_wait(eng, u):
            if u < NM:
                eng.wait_ge(got_wd[0], 16)
            elif u < D_EARLY:
                eng.wait_ge(got_wd[1], 16)
            else:
                eng.wait_ge(got_wd[2], 32)

        def clipped(eng, m, k):
            eng.wait_ge(bit_clip, 2 * (BIT_BASE[m] + k + 1))

        block = ctx.enter_context(nc.Block())

        @block.sync
        def _(sp):
            x_t = x.rearrange("(n p) h -> n p h", p=P)
            out_t = out.rearrange("(n p) h -> n p h", p=P)

            def load_x(n, s):
                sp.dma_start(xin[:, s, :], x_t[n, :, :]).then_inc(got_x[s], 16)

            def load_res(n, s):
                sp.dma_start(res[:, s, :], x_t[n, :, :]).then_inc(got_res[s], 16)

            def load_f(j):
                sp.dma_start(WF[:, NS + 2 * j + 1:NS + 2 * j + 3, :].rearrange("p u c -> p (u c)").bitcast(F32),
                             w_f[:, 1024 * j:1024 * (j + 1)]).then_inc(got_wf[j], 16)

            def load_bit(m, k):
                raw = BITS[m][k][0]
                if m == DOWN:
                    c0, c1 = DOWN_CHUNKS[k]
                    if c1 - c0 == 1:
                        sp.dma_start(raw, w_bd[P * c0:P * c0 + chunk_rows(c0), :]).then_inc(got_bit[m][k], 16)
                    else:
                        sp.dma_start(raw.rearrange("p (c h) -> p c h", h=H),
                                     w_bd[P * c0:P * c1, :].rearrange("(c p) h -> p c h", p=P)
                                     ).then_inc(got_bit[m][k], 16)
                else:
                    sp.dma_start(raw, (w_bu if m else w_bg)[P * k:P * (k + 1), :]).then_inc(got_bit[m][k], 16)

            sp.dma_start(h32[:, 0, :], x_t[0, :, :]).then_inc(got_first[0], 16)
            sp.dma_start(idf[:, :], ident).then_inc(got_ident, 16)
            sp.dma_start(sc[:, :], scal.partition_broadcast(P)).then_inc(got_scalars, 16)
            sp.dma_start(h32[:, 1, :], x_t[1, :, :]).then_inc(got_first[1], 16)
            for s in range(2):
                load_x(2 + s, s)
            sp.dma_start(WF[:, 1:NS + 1, :].rearrange("p u c -> p (u c)").bitcast(F32), w_s).then_inc(got_ws, 16)
            sp.dma_start(lp[:, :], local_point).then_inc(got_lp, 16)
            for what, *n in LOADS:
                if what == "f" and n[0] < NF - 1:
                    load_f(*n)
                elif what == "f":
                    tail = KC * F_TILES[-1][1]
                    sp.dma_start(WF[:, NS + 2 * NF - 1:NS + 2 * NF + 1, :].bitcast(F32)[:, :, 0:tail],
                                 w_f_tail.rearrange("p (u c) -> p u c", u=2)).then_inc(got_wf[NF - 1], 16)
                else:
                    if n == [DOWN, 3]:
                        sp.wait_ge(xq_tp, TT)
                    load_bit(*n)
            clipped(sp, GATE, PIECES[GATE] - 1)
            sp.dma_start(WD[:, 1:NM + 1, :].rearrange("p u c -> p (u c)").bitcast(F32), w_poly).then_inc(got_wd[0], 16)
            early = (D_EARLY - NM) * P
            sp.dma_start(WD[:, NM + 1:D_EARLY + 1, :].bitcast(F32),
                         w_down[0:early, :].rearrange("(c p) h -> p c h", p=P)).then_inc(got_wd[1], 16)
            clipped(sp, DOWN, PIECES[DOWN] - 1)
            for s in range(2):
                load_x(TT + s, s)
            sp.dma_start(WD[:, D_EARLY + 1:D_UNITS, :].bitcast(F32),
                         w_down[early:(NF - 1) * P, :].rearrange("(c p) h -> p c h", p=P)).then_inc(got_wd[2], 16)
            sp.dma_start(WD[0:D_UNIT_K[-1], D_UNITS, :].bitcast(F32), w_down[(NF - 1) * P:F, :]).then_inc(got_wd[2], 16)
            load_res(0, 0)
            load_res(1, 1)

            def down(b, front):
                for t in range(TT):
                    n = b * TT + t
                    if front and t < 2:
                        sp.wait_ge(xq_tp, TT * (b + 1) + t + 1)
                        load_x(TT * (b + 1) + t + 2, t)
                    sp.wait_ge(pair_free, PER_BLOCK * b + FIRST_D + t + 1)
                    sp.dma_start(out_t[n, :, :], res[:, t % 2, :]).then_inc(stored[t % 2], 16)
                    if front or t < TT - 2:
                        sp.wait_ge(stored[t % 2], 16 * (TT // 2) * b + 16 * (t // 2 + 1))
                        load_res(n + 2, t % 2)

            def next_x(b):
                for t in range(2):
                    sp.wait_ge(xq_tp, TT * b + t + 3)
                    load_x(TT * (b + 1) + t, t)

            with sp.Fori(0, NB - 2) as b:
                down(b, True)
                next_x(b + 1)
            down(NB - 2, True)
            down(NB - 1, False)
            for s in range(2):
                sp.wait_ge(stored[s], TOK // P // 2 * 16)

        @block.gpsimd
        def _(pool):
            pool.wait_ge(const_ready, 1)

            def rstd(n, t):
                pool.wait_ge(stats_v, STATS * n + STATS)
                nc.gpsimd.tensor_tensor(rs[:, t:t + 1], ve[:, t:t + 1], neghalf[:, :], ALU.pow).then_inc(rstd_ready, 1)

            def term_lo(b, m):
                pool.wait_ge(t_hi_ready, NM * b + m + 1)
                nc.gpsimd.tensor_tensor(t_lo[:, m, :], t32[:, m % 2, :], t_hi[:, m, :],
                                        ALU.subtract).then_inc(t_lo_ready, 1)

            def f_lo(b, j):
                rows = F_TILES[j][1]
                pool.wait_ge(h_hi_ready, NF * b + j + 1)
                nc.gpsimd.tensor_tensor(h_lo[0:rows, j, :], h32[0:rows, j % 2, :], h_hi[0:rows, j, :],
                                        ALU.subtract).then_inc(h_lo_ready, 1)

            def split_scale(n):
                tensor, u, cols, rows = UNITS[n]
                unit_wait(pool, n)
                raw = raw_unit(tensor, u, cols)[0:rows, :]
                nc.gpsimd.tensor_scalar(raw, raw, WS, 0.0, ALU.mult, ALU.add).then_inc(w_scaled, 1)

            def split_lo(n):
                tensor, u, cols, rows = UNITS[n]
                pool.wait_ge(w_hi, n + 1)
                nc.gpsimd.tensor_tensor(w_unit(tensor, u, 1, 0, cols)[0:rows, :],
                                        raw_unit(tensor, u, cols)[0:rows, :],
                                        w_unit(tensor, u, 0, 0, cols)[0:rows, :], ALU.subtract).then_inc(w_lo, 1)

            def scaled_ahead(units, u):
                k = units.index(u)
                return units[0:2] if k == 0 else units[k + 1:k + 2]

            def d_scale(u):
                d_unit_wait(pool, u)
                raw = raw_unit(WD, u)[0:D_UNIT_K[u], :]
                nc.gpsimd.tensor_scalar(raw, raw, WS, 0.0, ALU.mult, ALU.add).then_inc(wd_scaled, 1)

            def d_lo(u):
                rows = D_UNIT_K[u]
                pool.wait_ge(wd_hi, u + 1)
                nc.gpsimd.tensor_tensor(w_unit(WD, u, 1)[0:rows, :], raw_unit(WD, u)[0:rows, :],
                                        w_unit(WD, u, 0)[0:rows, :], ALU.subtract).then_inc(wd_lo, 1)

            def bit_total(m):
                cols = slice(BIT_BASE[m], BIT_BASE[m] + PIECES[m])
                pool.wait_ge(bit_abs, BIT_BASE[m] + PIECES[m])
                nc.gpsimd.partition_all_reduce(wtot[:, cols], wabs[:, cols], P, RADD).then_inc(bit_tot, 1)

            def bit_rounding(m, k):
                raw, _, rows = BITS[m][k]
                pool.wait_ge(bit_mean, BIT_MEANS * (m + 1))
                nc.gpsimd.tensor_scalar(raw, raw, rw[0:rows, m:m + 1], MAGIC, ALU.mult,
                                        ALU.add).then_inc(bit_round[m], 1)

            def up(b, order, prep):
                for i, (kind, n) in enumerate(order):
                    if kind == "S" and prep is not no_prep:
                        prep(PREP_FIRST)
                        term_lo(b, 0)
                    elif kind == "S":
                        for m in range(NM):
                            term_lo(b, m)
                    first, rest = halves(PREP.get(i, []))
                    prep(first)
                    if kind == "F":
                        f_lo(b, n)
                    prep(rest)

            def prep(steps):
                for what, *n in steps:
                    if what == "sum" and n[1] == PIECES[n[0]] - 1:
                        bit_total(n[0])
                    elif what == "round":
                        bit_rounding(*n)
                    elif what == "term":
                        term_lo(0, *n)
                    elif what == "split" and n[0] in POOL_SPLIT:
                        for u in scaled_ahead(POOL_SPLIT, n[0]):
                            split_scale(u)
                        split_lo(*n)
                    elif what == "d" and n[0] in POOL_D:
                        for u in scaled_ahead(POOL_D, n[0]):
                            d_scale(u)
                        d_lo(*n)

            nc.gpsimd.memset(wabs[:, NPIECES - 1:NPIECES], 0.0).then_inc(tail_zero, 1)
            for t in range(TT):
                rstd(t, t)
            up(0, FIRST, prep)
            with pool.Fori(0, NB - 1) as b:
                for t in range(TT):
                    rstd((b + 1) * TT + t, t)
                up(b + 1, STEADY, no_prep)

        @block.scalar
        def _(act):
            def front_abs(b, t):
                n = b * TT + t
                act.wait_ge(xn_ready, n + 1)
                if isinstance(b, int) and b == 0:
                    unused = t_hi[:, t, :]
                else:
                    act.wait_ge(xq_tp, n - 1)
                    unused = xq[:, t % 2, :]
                nc.scalar.activation(unused, x_buffer(b, t), ACT.Abs,
                                     accum_out=xabs[:, t:t + 1]).then_inc(xabs_ready, 1)

            def front_split_hi(b, t):
                n = b * TT + t
                act.wait_ge(xn_ready, n + 1)
                if t >= 2:
                    act.wait_ge(x_tp, n - 1)
                nc.scalar.copy(x_part(t, 0), x_buffer(b, t)).then_inc(xs_hi, 1)

            def front_hi(b, t):
                n = b * TT + t
                act.wait_ge(x_tp, n + 1)
                if isinstance(b, int) and b == 0:
                    source = FIRST_X[t][:, :]
                else:
                    source = tpX_h[:, 0:H]
                nc.scalar.copy(xT_hi[:, :, P * t:P * (t + 1)],
                               source.rearrange("p (k t) -> p k t", k=KC)).then_inc(xhi_ready, 1)

            def front_q(b, t):
                if isinstance(b, int) and b == 0:
                    bank = FIRST_XQ[t]
                    act.wait_ge(xq_tp, t // 2 * 2 + 2)
                else:
                    bank = tpQ[:, 0:KC * P]
                    act.wait_ge(xq_tp, b * TT + t + 1)
                nc.scalar.copy(xqT[:, :, P * t:P * (t + 1)],
                               bank.rearrange("p (k t) -> p k t", k=KC)).then_inc(xqT_ready, 1)

            def split_hi(n):
                tensor, u, cols, rows = UNITS[n]
                unit_wait(act, n)
                if n:
                    act.wait_ge(w_lo, n)
                to, raw = w_unit(tensor, u, 0, 0, cols)[0:rows, :], raw_unit(tensor, u, cols)[0:rows, :]
                if n in POOL_SPLIT:
                    act.wait_ge(w_scaled, POOL_SPLIT.index(n) + 1)
                    nc.scalar.copy(to, raw).then_inc(w_hi, 1)
                else:
                    nc.scalar.mul(to, raw, WS).then_inc(w_hi, 1)

            def d_hi(u):
                d_unit_wait(act, u)
                if u:
                    act.wait_ge(wd_lo, u)
                rows = D_UNIT_K[u]
                if u in POOL_D:
                    act.wait_ge(wd_scaled, POOL_D.index(u) + 1)
                    nc.scalar.copy(w_unit(WD, u, 0)[0:rows, :], raw_unit(WD, u)[0:rows, :]).then_inc(wd_hi, 1)
                else:
                    nc.scalar.mul(w_unit(WD, u, 0)[0:rows, :], raw_unit(WD, u)[0:rows, :], WS).then_inc(wd_hi, 1)

            def bit_sum(m, k):
                raw, dst, rows = BITS[m][k]
                n = BIT_BASE[m] + k
                act.wait_ge(got_bit[m][k], 16)
                if n == NPIECES - 1:
                    act.wait_ge(tail_zero, 1)
                nc.scalar.activation(dst, raw, ACT.Abs, accum_out=wabs[0:rows, n:n + 1]).then_inc(bit_abs, 1)

            def term_hi(b, m):
                act.wait_ge(term_ready, NM * b + m + 1)
                nc.scalar.copy(t_hi[:, m, :], t32[:, m % 2, :]).then_inc(t_hi_ready, 1)

            def f_gate(b, j, i):
                rows = F_TILES[j][1]
                act.wait_ge(pair_ready, PER_BLOCK * b + i + 1)
                nc.scalar.activation(half[0:rows, i % RING, 0:BLK], bankA[i % RING][0:rows, 0:BLK], ACT.Silu,
                                     scale=1.0 / WS).then_inc(half_ready, 1)

            def f_hi(b, j, i):
                rows = F_TILES[j][1]
                act.wait_ge(pair_free, PER_BLOCK * b + i + 1)
                nc.scalar.copy(h_hi[0:rows, j, :], h32[0:rows, j % 2, :]).then_inc(h_hi_ready, 1)

            def b_gate(b, n, i):
                c = n % NC
                cols = B_COLS[c][1]
                act.wait_ge(pair_ready, PER_BLOCK * b + i + 1)
                nc.scalar.activation(half[:, i % RING, 0:cols], bankA[i % RING][:, 0:cols], ACT.Relu,
                                     scale=wsc[:, 0:1]).then_inc(relu_ready, 1)
                act.wait_ge(relu_ready, TT * NC * b + n + 1)
                nc.scalar.activation(half[:, i % RING, 0:cols], half[:, i % RING, 0:cols],
                                     ACT.Square).then_inc(half_ready, 1)

            def b_round(b, t):
                act.wait_ge(bit_v, BIT * (b * TT + t) + BIT_SCALED)
                nc.scalar.activation(prod, prod, ACT.Copy, bias=MAGIC, scale=qs[:, 0:1]).then_inc(q8_round, 1)

            def up(b, order, prep):
                due = None
                for i, (kind, n) in enumerate(order):
                    first, rest = halves(PREP.get(i, []))
                    if kind == "S" and prep is not no_prep:
                        prep(PREP_FIRST)
                        term_hi(b, 0)
                    elif kind == "S":
                        for m in range(NM):
                            term_hi(b, m)
                    elif kind == "F":
                        f_gate(b, n, i)
                    else:
                        b_gate(b, n, i)
                    if due is not None:
                        b_round(b, due)
                        due = None
                    prep(first)
                    if kind == "F":
                        f_hi(b, n, i)
                    prep(rest)
                    if kind == "B" and n % NC == NC - 1:
                        due = n // NC
                b_round(b, due)

            def down(b, front):
                for t in range(TT):
                    n = b * TT + t
                    act.wait_ge(q8_tp, n + 1)
                    nc.scalar.copy(q8T[:, 0:NQ1, :], tpX_b.rearrange("p (c t) -> p c t", t=P))
                    nc.scalar.copy(q8T[:, NQ1:NI - 1, :],
                                   tpQ[:, 0:(NI - 1 - NQ1) * P].rearrange("p (c t) -> p c t", t=P))
                    nc.scalar.copy(q8T[0:I_CHUNKS[-1][1], NI - 1, :],
                                   tpQ[0:I_CHUNKS[-1][1], (NI - 1 - NQ1) * P:(NI - NQ1) * P]).then_inc(q8T_ready, 1)
                    if front:
                        front_split_hi(b + 1, t)
                        front_abs(b + 1, t)
                        front_hi(b + 1, t)
                        front_q(b + 1, t)

            act.wait_ge(got_ident, 16)
            nc.scalar.copy(idb[:, :], idf[:, :]).then_inc(idb_ready, 1)
            act.wait_ge(expo_ready, 2)
            nc.scalar.activation(ratio[:, :], expo[:, :], ACT.Exp).then_inc(ratio_ready, 1)
            act.wait_ge(const_ready, 1)
            nc.scalar.activation(warm[:, :], neghalf[:, :], ACT.Silu)
            front_abs(0, 0)
            front_hi(0, 0)
            split_hi(0)
            front_hi(0, 1)
            front_abs(0, 1)
            front_hi(0, 2)
            front_abs(0, 2)
            front_hi(0, 3)
            split_hi(1)
            front_abs(0, 3)

            act.wait_ge(x_tp, TT)
            nc.scalar.copy(idh, idb[:, :]).then_inc(idh_ready, 1)

            def prep(steps):
                for what, *n in steps:
                    if what == "split":
                        split_hi(*n)
                    elif what == "d":
                        d_hi(*n)
                    elif what == "sum":
                        bit_sum(*n)
                    elif what == "xq":
                        front_q(0, *n)
                    elif what == "term":
                        term_hi(0, *n)

            up(0, FIRST, prep)
            with act.Fori(0, NB - 1) as b:
                down(b, True)
                up(b + 1, STEADY, no_prep)
            down(NB - 1, False)

        @block.vector
        def _(dve):
            def front_stats(b, t):
                n = b * TT + t
                one = slice(t, t + 1)

                def step(k, ins):
                    ins.then_inc(stats_v, 1)
                    dve.wait_ge(stats_v, STATS * n + k)

                if not (isinstance(b, int) and b == 0):
                    dve.wait_ge(got_x[t % 2], 16 * (TT // 2) * b + 16 * (t // 2))
                elif t < 2:
                    dve.wait_ge(got_first[t], 16)
                else:
                    dve.wait_ge(got_x[t - 2], 16)
                step(1, nc.vector.bn_stats(st6[:, :], x_buffer(b, t)))
                nc.vector.memset(unused[:, :], 0.0)
                step(2, nc.vector.bn_aggr(mv[:, t, :], st6[:, :]))
                nc.vector.tensor_scalar_add(ve[:, one], mv[:, t, 1:2], LN_EPS).then_inc(stats_v, 1)

            def front_xn(b, t):
                xt = x_buffer(b, t)
                dve.wait_ge(rstd_ready, b * TT + t + 1)
                nc.vector.tensor_scalar(xt, xt, mv[:, t, 0:1], rs[:, t:t + 1], ALU.subtract,
                                        ALU.mult).then_inc(xn_ready, 1)

            def front_quant(b, t):
                n = b * TT + t
                one = slice(t, t + 1)
                tmp = t32[:, t % 2, :]
                if isinstance(b, int) and b == 0:
                    tmp = h_lo[:, 6:8, :].rearrange("p j t -> p (j t)").bitcast(F32)

                def step(k, ins):
                    ins.then_inc(quant_v, 1)
                    dve.wait_ge(quant_v, QUANT * n + k)

                dve.wait_ge(xabs_ready, n + 1)
                nc.vector.tensor_scalar_mul(beta[:, one], xabs[:, one], 1.0 / H)
                step(1, nc.vector.tensor_scalar(beta_e[:, one], xabs[:, one], 1.0 / H, Q_EPS, ALU.mult, ALU.add))
                step(2, nc.vector.reciprocal(rbeta[:, one], beta_e[:, one]))
                step(3, nc.vector.tensor_scalar(tmp, x_buffer(b, t), rbeta[:, one], SQRT7, ALU.mult, ALU.mult))
                step(4, nc.vector.tensor_scalar(tmp, tmp, MAGIC, MAGIC - 8.0, ALU.add, ALU.max))
                nc.vector.tensor_scalar(xq_buffer(b, t), tmp, MAGIC + 7.0, MAGIC, ALU.min,
                                        ALU.subtract).then_inc(quant_v, 1)

            def front_split_lo(b, t):
                dve.wait_ge(xs_hi, (b - 1) * TT + t + 1)
                nc.vector.tensor_tensor(x_part(t, 1), x_buffer(b, t), x_part(t, 0), ALU.subtract).then_inc(xs_lo, 1)

            def front_lo(b, t):
                dve.wait_ge(xhi_ready, b * TT + t + 1)
                to = xT_lo[:, :, P * t:P * (t + 1)]
                if isinstance(b, int) and b == 0:
                    nc.vector.tensor_tensor(to, FIRST_X[t][:, :].rearrange("p (k t) -> p k t", k=KC),
                                            xT_hi[:, :, P * t:P * (t + 1)], ALU.subtract).then_inc(xlo_ready, 1)
                else:
                    nc.vector.tensor_copy(to, tpX_h[:, H:2 * H].rearrange("p (k t) -> p k t", k=KC)
                                          ).then_inc(xlo_ready, 1)

            def split_lo(n):
                tensor, u, cols, rows = UNITS[n]
                dve.wait_ge(w_hi, n + 1)
                nc.vector.scalar_tensor_tensor(w_unit(tensor, u, 1, 0, cols)[0:rows, :],
                                               raw_unit(tensor, u, cols)[0:rows, :], WS,
                                               w_unit(tensor, u, 0, 0, cols)[0:rows, :],
                                               ALU.mult, ALU.subtract).then_inc(w_lo, 1)

            def d_lo(u):
                rows = D_UNIT_K[u]
                dve.wait_ge(wd_hi, u + 1)
                nc.vector.scalar_tensor_tensor(w_unit(WD, u, 1)[0:rows, :], raw_unit(WD, u)[0:rows, :], WS,
                                               w_unit(WD, u, 0)[0:rows, :], ALU.mult,
                                               ALU.subtract).then_inc(wd_lo, 1)

            def bit_means(m):
                one = slice(m, m + 1)
                count = I * H

                def step(k, ins):
                    ins.then_inc(bit_mean, 1)
                    dve.wait_ge(bit_mean, BIT_MEANS * m + k)

                dve.wait_ge(bit_tot, m + 1)
                step(1, nc.vector.tensor_reduce(wsum[:, one], wtot[:, BIT_BASE[m]:BIT_BASE[m] + PIECES[m]],
                                                AX_X, ALU.add))
                nc.vector.tensor_scalar_mul(wmean[:, one], wsum[:, one], 1.0 / count).then_inc(bit_mean, 1)
                step(3, nc.vector.tensor_scalar(wmean_e[:, one], wsum[:, one], 1.0 / count, Q_EPS, ALU.mult,
                                                ALU.add))
                nc.vector.tensor_tensor(wsc[:, one], wmean[:, one], sc[:, one], ALU.mult)
                nc.vector.reciprocal(rw[:, one], wmean_e[:, one]).then_inc(bit_mean, 1)

            def bit_clipping(m, k):
                raw, dst, _ = BITS[m][k]
                dve.wait_ge(bit_round[m], k + 1)
                nc.vector.tensor_scalar(dst, raw, MAGIC, 1.0, ALU.subtract, ALU.min).then_inc(bit_clip, 1)
                dve.wait_ge(bit_clip, 2 * (BIT_BASE[m] + k) + 1)
                nc.vector.tensor_scalar_max(dst, dst, -1.0).then_inc(bit_clip, 1)

            def first_term(b, i):
                a, g = bankA[i % RING], bankB[i % RING]
                dve.wait_ge(pair_ready, PER_BLOCK * b + i + 1)
                nc.vector.tensor_scalar_mul(t32[:, 0, :], a[:, :], 1.0 / WS).then_inc(term_ready, 1)
                nc.vector.tensor_scalar(delta[:, :], g[:, :], 1.0 / WS, lp[:, 0:1], ALU.mult,
                                        ALU.subtract).then_inc(pair_free, 1)
                dve.wait_ge(pair_free, PER_BLOCK * b + i + 1)

            def term(b, m):
                if m == 5:
                    dve.wait_ge(term_ready, NM * b + m)
                    nc.vector.scalar_tensor_tensor(delta[:, :], delta[:, :], THD, delta[:, :], ALU.is_le,
                                                   ALU.mult).then_inc(keep_v, 1)
                    dve.wait_ge(keep_v, 2 * b + 1)
                    nc.vector.scalar_tensor_tensor(delta[:, :], delta[:, :], -THD, delta[:, :], ALU.is_ge,
                                                   ALU.mult).then_inc(keep_v, 1)
                    dve.wait_ge(keep_v, 2 * b + 2)
                dve.wait_ge(term_ready, NM * b + m)
                if m >= 2:
                    dve.wait_ge(t_lo_ready, NM * b + m - 1)
                nc.vector.scalar_tensor_tensor(t32[:, m % 2, :], delta[:, :], ratio[:, m - 1:m],
                                               t32[:, (m - 1) % 2, :], ALU.mult,
                                               ALU.mult).then_inc(term_ready, 1)

            def f_product(b, j, i):
                rows = F_TILES[j][1]
                dve.wait_ge(half_ready, half_count(b, i))
                if j >= 2:
                    dve.wait_ge(h_lo_ready, NF * b + j - 1)
                nc.vector.scalar_tensor_tensor(h32[0:rows, j % 2, :], bankB[i % RING][0:rows, :], 1.0 / WS,
                                               half[0:rows, i % RING, :], ALU.mult, ALU.mult).then_inc(pair_free, 1)

            def half_count(b, i):
                return (NF + TT * NC) * b + i

            def b_product(b, n, i):
                o, cols = B_COLS[n % NC]
                dve.wait_ge(half_ready, half_count(b, i))
                nc.vector.tensor_tensor(prod[:, o:o + cols], bankB[i % RING][:, 0:cols],
                                        half[:, i % RING, 0:cols], ALU.mult).then_inc(pair_free, 1)
                if n % NC == NC - 1:
                    dve.wait_ge(pair_free, PER_BLOCK * b + i + 1)
                    b_scale(b, n // NC)

            def b_scale(b, t):
                def step(k, ins):
                    ins.then_inc(bit_v, 1)
                    dve.wait_ge(bit_v, BIT * (b * TT + t) + k)

                bt = beta[:, t:t + 1]
                nc.vector.tensor_tensor(b2[:, :], bt, bt, ALU.mult).then_inc(bit_v, 1)
                step(2, nc.vector.tensor_reduce(pmax[:, :], prod, AX_X, ALU.max, apply_absolute_value=True))
                step(3, nc.vector.scalar_tensor_tensor(cB[:, :], bt, wsc[:, 1:2], b2[:, :], ALU.mult, ALU.mult))
                step(4, nc.vector.scalar_tensor_tensor(cBa[:, :], cB[:, :], -1.0, cB[:, :], ALU.mult, ALU.max))
                nc.vector.tensor_tensor(gam[:, :], cBa[:, :], pmax[:, :], ALU.mult)
                step(5, nc.vector.tensor_scalar(game[:, :], cBa[:, :], pmax[:, :], Q_EPS, ALU.mult, ALU.add))
                nc.vector.tensor_scalar(od[:, t:t + 1], gam[:, :], 1.0 / 127.0, wsc[:, 2:3], ALU.mult, ALU.mult)
                step(6, nc.vector.reciprocal(rgam[:, :], game[:, :]))
                step(7, nc.vector.tensor_scalar(qs[:, :], rgam[:, :], 127.0, cB[:, :], ALU.mult, ALU.mult))

            def b_store(b, t):
                base = BIT * (b * TT + t)
                dve.wait_ge(q8_round, b * TT + t + 1)
                nc.vector.tensor_scalar(q8[:, t, :], prod, MAGIC, 127.0, ALU.subtract, ALU.min).then_inc(bit_v, 1)
                dve.wait_ge(bit_v, base + 8)
                nc.vector.tensor_scalar_max(q8[:, t, :], q8[:, t, :], -128.0).then_inc(bit_v, 1)

            def up(b, order, prep):
                for i, (kind, n) in enumerate(order):
                    steps = PREP.get(i, [])
                    if kind == "S" and prep is not no_prep:
                        prep(PREP_FIRST)
                        first_term(b, i)
                    elif kind == "S":
                        first_term(b, i)
                        for m in range(1, NM):
                            term(b, m)
                    elif kind == "F":
                        f_product(b, n, i)
                    else:
                        if n % NC == 0 and n > 0:
                            prep(steps)
                            steps = []
                            b_store(b, n // NC - 1)
                            dve.wait_ge(bit_v, BIT * (b * TT + n // NC) - 1)
                        b_product(b, n, i)
                    prep(steps)

            def down(b, is_front):
                for t in range(TT):
                    n = b * TT + t
                    i = FIRST_D + t
                    if is_front:
                        front_stats(b + 1, t)
                        front_xn(b + 1, t)
                    if t == 0:
                        b_store(b, TT - 1)
                    if is_front:
                        front_split_lo(b + 1, t)
                        front_quant(b + 1, t)
                        front_lo(b + 1, t)
                    dve.wait_ge(got_res[t % 2], 16 * (TT // 2) * b + 16 * (t // 2 + 1))
                    dve.wait_ge(float_ready, n + 1)
                    nc.vector.scalar_tensor_tensor(res[:, t % 2, :], bankA[i % RING][:, :], 1.0 / WS,
                                                   res[:, t % 2, :], ALU.mult, ALU.add).then_inc(out_v, 1)
                    dve.wait_ge(out_v, n + 1)
                    dve.wait_ge(pair_ready, PER_BLOCK * b + i + 1)
                    nc.vector.scalar_tensor_tensor(res[:, t % 2, :], bankB[i % RING][:, :], od[:, t:t + 1],
                                                   res[:, t % 2, :], ALU.mult, ALU.add).then_inc(pair_free, 1)

            nc.vector.memset(neghalf[:, :], -0.5).then_inc(const_ready, 1)
            nc.vector.memset(h_hi[:, 0, :], 0.0).then_inc(zeros_ready, 1)
            front_stats(0, 0)
            dve.wait_ge(got_scalars, 16)
            nc.vector.tensor_scalar_mul(expo[:, 0:1], sc[:, 3:4], -1.0).then_inc(expo_ready, 1)
            nc.vector.tensor_tensor(expo[:, 1:G], sc[:, 3:2 + G], sc[:, 4:3 + G], ALU.subtract).then_inc(expo_ready, 1)
            for t in range(1, TT):
                front_stats(0, t)
                front_xn(0, t - 1)
            front_lo(0, 0)
            front_xn(0, TT - 1)
            front_lo(0, 1)
            split_lo(0)
            front_lo(0, 2)
            front_lo(0, 3)
            split_lo(1)
            dve.wait_ge(ratio_ready, 1)
            dve.wait_ge(got_lp, 16)

            def prep(steps):
                for what, *n in steps:
                    if what == "split" and n[0] not in POOL_SPLIT:
                        split_lo(*n)
                    elif what == "d" and n[0] not in POOL_D:
                        d_lo(*n)
                    elif what == "mean":
                        bit_means(*n)
                    elif what == "clip":
                        bit_clipping(*n)
                    elif what == "quant":
                        front_quant(0, *n)
                    elif what == "term":
                        term(0, *n)

            up(0, FIRST, prep)
            with dve.Fori(0, NB - 1) as b:
                down(b, True)
                up(b + 1, STEADY, no_prep)
            down(NB - 1, False)

        @block.tensor
        def _(pe):
            def split_product(bank, w, xx, ks, last_of_all=True, first=True):
                for k in ks:
                    for wp, xp in ((0, 0), (0, 1), (1, 0)):
                        ins = nc.tensor.matmul(bank, w(wp, k), xx(xp, k),
                                               start=(first and k == ks[0] and (wp, xp) == (0, 0)),
                                               stop=(last_of_all and k == ks[-1] and wp == 1))
                return ins

            def xT(part, k):
                return (xT_lo if part else xT_hi)[:, k, :]

            def free(b, i):
                if not (isinstance(b, int) and PER_BLOCK * b + i < RING):
                    pe.wait_ge(pair_free, PER_BLOCK * b + i - RING + 1)

            def x_transposes(b, t):
                if isinstance(b, int) and b == 0:
                    pe.wait_ge(xn_ready, t + 1)
                    for k in range(KC):
                        ins = nc.tensor.transpose(FIRST_X[t][:, P * k:P * (k + 1)],
                                                  x_buffer(b, t)[:, P * k:P * (k + 1)], idf[:, :])
                else:
                    pe.wait_ge(xs_lo, (b - 1) * TT + t + 1)
                    for part in range(2):
                        for k in range(KC):
                            ins = nc.tensor.transpose(tpX_h[:, H * part + P * k:H * part + P * (k + 1)],
                                                      x_part(t, part)[:, P * k:P * (k + 1)], idh)
                ins.then_inc(x_tp, 1)

            def xq_transposes(b, t):
                pe.wait_ge(quant_v, QUANT * (b * TT + t) + QUANT)
                bank = FIRST_XQ[t] if isinstance(b, int) and b == 0 else tpQ[:, 0:KC * P]
                for k in range(KC):
                    ins = nc.tensor.transpose(bank[:, P * k:P * (k + 1)], xq_buffer(b, t)[:, P * k:P * (k + 1)], idb[:, :])
                ins.then_inc(xq_tp, 1)

            def s_pair(b, i):
                free(b, i)
                for side, bank in ((0, bankA[i % RING]), (1, bankB[i % RING])):
                    for part, passes in ((0, ((0, 0), (1, 0))), (1, ((0, 1),))):
                        if side == 0:
                            pe.wait_ge(xlo_ready if part else xhi_ready, TT * (b + 1))
                        if part == 0:
                            pe.wait_ge(w_lo, side + 1)
                        for k in range(KC):
                            for wp, xp in passes:
                                ins = nc.tensor.matmul(bank[:, :], w_unit(WF, side, wp, P * k, P), xT(xp, k),
                                                       start=(part == 0 and k == 0 and wp == 0),
                                                       stop=(part == 1 and k == KC - 1))
                ins.then_inc(pair_ready, 1)

            def f_pair(b, j, i, first_use):
                n = F_TILES[j][1]
                free(b, i)
                if first_use:
                    pe.wait_ge(w_lo, U_F + 2 * j + 2)
                split_product(bankA[i % RING][0:n, :], lambda q, k: w_unit(WF, NS + 2 * j, q, n * k, n), xT, range(KC))
                split_product(bankB[i % RING][0:n, :], lambda q, k: w_unit(WF, NS + 2 * j + 1, q, n * k, n), xT,
                              range(KC)).then_inc(pair_ready, 1)

            def b_pair(b, m, i, first_use):
                t = m // NC
                o, n = B_COLS[m % NC]
                free(b, i)
                if m == 0:
                    pe.wait_ge(xqT_ready, TT * (b + 1))
                    if first_use:
                        clipped(pe, UP, PIECES[UP] - 1)
                for side, bank in ((0, bankA[i % RING]), (1, bankB[i % RING])):
                    for k in range(KC):
                        ins = nc.tensor.matmul(bank[:, 0:n], xqT[:, k, P * t:P * (t + 1)],
                                               WB[:, side, I * k + o:I * k + o + n],
                                               start=(k == 0), stop=(k == KC - 1))
                ins.then_inc(pair_ready, 1)

            def up(b, order, first_use):
                for i, (kind, n) in enumerate(order):
                    if kind == "S":
                        s_pair(b, i)
                    elif kind == "F":
                        f_pair(b, n, i, first_use)
                    else:
                        b_pair(b, n, i, first_use)
                    if first_use and i in (2, 4):
                        for t in (i - 2, i - 1):
                            xq_transposes(b, t)

            def down(b, front, first_use=False):
                for t in range(TT):
                    n = b * TT + t
                    i = FIRST_D + t
                    free(b, i)
                    tok = slice(P * t, P * (t + 1))

                    def act_part(q, u):
                        if u < NM:
                            return (t_lo if q else t_hi)[:, u, tok]
                        kk = F_TILES[u - NM][1]
                        return (h_lo if q else h_hi)[0:kk, u - NM, tok]

                    def w_part(q, u):
                        return w_unit(WD, u, q)[0:D_UNIT_K[u], :]

                    if t == 0:
                        pe.wait_ge(t_lo_ready, NM * (b + 1))
                    bank = bankA[i % RING][:, :]
                    for u in range(NM):
                        if first_use and t == 0:
                            pe.wait_ge(wd_lo, u + 1)
                        split_product(bank, act_part, w_part, [u], last_of_all=False, first=(u == 0))
                    pe.wait_ge(bit_v, BIT * n + BIT)
                    if front or t == 0:
                        pe.wait_ge(xlo_ready, n + TT)
                        pe.wait_ge(xqT_ready, n + TT)
                    for c, (o, kk) in enumerate(I_CHUNKS):
                        to = tpX_b[0:kk, P * c:P * (c + 1)] if c < NQ1 else tpQ[0:kk, P * (c - NQ1):P * (c - NQ1 + 1)]
                        ins = nc.tensor.transpose(to, q8[:, t, o:o + kk], idb[:, :])
                    ins.then_inc(q8_tp, 1)
                    if t == 0:
                        pe.wait_ge(h_lo_ready, NF * (b + 1))
                    for u in range(NM, D_UNITS):
                        if first_use and t == 0:
                            pe.wait_ge(wd_lo, u + 1)
                        ins = split_product(bank, act_part, w_part, [u], last_of_all=(u == D_UNITS - 1), first=False)
                    ins.then_inc(float_ready, 1)
                    pe.wait_ge(q8T_ready, n + 1)
                    if front:
                        x_transposes(b + 1, t)
                        xq_transposes(b + 1, t)
                    if first_use and t == 0:
                        clipped(pe, DOWN, PIECES[DOWN] - 1)
                    for c, (o, kk) in enumerate(I_CHUNKS):
                        ins = nc.tensor.matmul(bankB[i % RING][:, :], q8T[0:kk, c, :], WBD[0:kk, c, :],
                                               start=(c == 0), stop=(c == NI - 1))
                    ins.then_inc(pair_ready, 1)

            def warm_up(n):
                for _ in range(n):
                    nc.tensor.matmul(bankB[2][:, :], h_hi[:, 0, 0:P], h_hi[:, 0, :], start=True, stop=True)

            pe.wait_ge(zeros_ready, 1)
            warm_up(12)
            pe.wait_ge(got_ident, 16)
            for t in range(TT):
                x_transposes(0, t)
                warm_up(2)
            pe.wait_ge(idb_ready, 1)
            up(0, FIRST, True)
            pe.wait_ge(idh_ready, 1)
            down(0, True, True)
            up(1, STEADY, False)
            with pe.Fori(1, NB - 1) as b:
                down(b, True)
                up(b + 1, STEADY, False)
            down(NB - 1, False)


def kernel(**inputs):
    import numpy as np
    import concourse.bacc as bacc
    from concourse.bass_utils import run_bass_kernel_spmd

    def get(name):
        return np.asarray(inputs["L0_" + name])

    x = get("attn_hidden_states")
    B, T, H = x.shape
    KC = H // P

    def chunked(w):
        return w.T.reshape(KC, P, w.shape[0]).transpose(1, 0, 2)

    def flat(*parts):
        return np.ascontiguousarray(np.concatenate([a.reshape(a.shape[0], -1) for a in parts], axis=1))

    gate, up = chunked(get("attn_ffn_gate_w")), chunked(get("attn_ffn_up_w"))
    F = gate.shape[2]
    whole = F // P * P
    fuse = get("attn_fuse_weight")
    arrays = {
        "x": np.ascontiguousarray(x.reshape(B * T, H)),
        "w_s": flat(chunked(get("attn_up_w")), chunked(get("attn_gate_w"))),
        "w_f": flat(*[w[:, :, o:o + P] for o in range(0, whole, P) for w in (gate, up)]),
        "w_f_tail": flat(gate[:, :, whole:], up[:, :, whole:]),
        "w_poly": flat(get("attn_local_approx_output").T, fuse.transpose(1, 2, 0)),
        "w_down": np.ascontiguousarray(get("attn_ffn_down_w").T),
        "w_bg": np.ascontiguousarray(get("ffn_w_gate").T),
        "w_bu": np.ascontiguousarray(get("ffn_w_up").T),
        "w_bd": np.ascontiguousarray(get("ffn_w_down").T),
        "local_point": np.ascontiguousarray(get("attn_local_point").reshape(-1, 1)),
        "scal": np.concatenate([get("ffn_s_gate"), get("ffn_s_up"), get("ffn_s_down"),
                                get("attn_discount_factor")]),
        "ident": np.eye(P, dtype=np.float32),
    }
    nc = bacc.Bacc("TRN2", target_bir_lowering=False, num_devices=1)
    arrays = {"in_" + n: a for n, a in arrays.items()}
    args = [nc.dram_tensor(n, a.shape, mybir.dt.from_np(a.dtype), kind="ExternalInput").ap()
            for n, a in arrays.items()]
    args.append(nc.dram_tensor("y", (B * T, H), F32, kind="ExternalOutput").ap())
    bass_kernel(nc, *args)
    r = run_bass_kernel_spmd(nc, [arrays], core_ids=[0])
    return r.results[0]["y"].reshape(B, T, H)
```
